# Optimizing a Trainium2 kernel written in Bass

```python
import numpy as np
import jax
import jax.numpy as jnp

def _softmax(x, axis=-1):
    return jax.nn.softmax(x, axis=axis)

def _gelu(x):
    return jax.nn.gelu(x, approximate=True)

def _silu(x):
    return jax.nn.silu(x)

def _sigmoid(x):
    return jax.nn.sigmoid(x)

def _layernorm(x, axis=-1, eps=1e-05):
    m = jnp.mean(x, axis=axis, keepdims=True)
    v = jnp.var(x, axis=axis, keepdims=True)
    return (x - m) / jnp.sqrt(v + eps)

def _scatter_add(tgt, idx, src, axis=0):
    return tgt.at[idx].add(src)

def _segment_sum(src, seg, n):
    return jax.ops.segment_sum(src, seg, n)
kernel_name = 'mk_recurrent_d1_jaxref_r4_5c5fb3'

def setup_inputs(seed: int=0):
    np.random.seed(seed)
    _w = jnp.asarray

    def _L0_attn_setup():
        import jax, jax.numpy as jnp
        import numpy as np
        D_INNER, D_STATE, DT_RANK = (256, 16, 32)

        def _selective_scan(x, x_proj_w, dt_proj_w, dt_proj_b, A_log, Dp):
            A = -jnp.exp(A_log)
            dbc = jnp.einsum('bld,nd->bln', x, x_proj_w)
            delta, Bm, Cm = jnp.split(dbc, [DT_RANK, DT_RANK + D_STATE], axis=-1)
            delta = jax.nn.softplus(jnp.einsum('blr,dr->bld', delta, dt_proj_w) + dt_proj_b)
            deltaA = jnp.exp(delta[..., None] * A)
            BX = delta[..., None] * Bm[:, :, None, :] * x[..., None]

            def comb(e1, e2):
                a1, b1 = e1
                a2, b2 = e2
                return (a2 * a1, a2 * b1 + b2)
            _, hs = jax.lax.associative_scan(comb, (deltaA, BX), axis=1)
            y = jnp.einsum('blds,bls->bld', hs, Cm)
            return y + Dp * x
        key = jax.random.key(seed)
        ks = jax.random.split(key, 12)
        B, L = (4, 512)
        A_row = jnp.log(jnp.arange(1, D_STATE + 1, dtype=jnp.float32))
        A_log = jnp.tile(A_row[None, :], (D_INNER, 1))
        s = 0.02
        return {'x': jax.random.normal(ks[0], (B, L, D_INNER), jnp.float32), 'x_proj_w': jax.random.normal(ks[1], (DT_RANK + 2 * D_STATE, D_INNER), jnp.float32) * s, 'dt_proj_w': jax.random.normal(ks[2], (D_INNER, DT_RANK), jnp.float32) * DT_RANK ** (-0.5), 'dt_proj_b': jax.random.normal(ks[3], (D_INNER,), jnp.float32) * 0.1 - 4.0, 'A_log': A_log, 'D': jnp.ones((D_INNER,), jnp.float32), 'x_proj_b_w': jax.random.normal(ks[4], (DT_RANK + 2 * D_STATE, D_INNER), jnp.float32) * s, 'dt_proj_b_w': jax.random.normal(ks[5], (D_INNER, DT_RANK), jnp.float32) * DT_RANK ** (-0.5), 'dt_proj_b_b': jax.random.normal(ks[6], (D_INNER,), jnp.float32) * 0.1 - 4.0, 'A_b_log': A_log, 'D_b': jnp.ones((D_INNER,), jnp.float32)}
    _L0_attn_in = _L0_attn_setup()

    def _L0_ffn_setup():
        import jax, jax.numpy as jnp
        import numpy as np
        B, S, H = (8, 1024, 256)
        NAV = 128
        E = 8
        F = 2 * H
        key = jax.random.key(seed)
        ks = jax.random.split(key, 12)

        def w(k, shape, fan_in):
            return jax.random.normal(k, shape, dtype=jnp.float32) / np.sqrt(fan_in)
        return {'hidden_states': jax.random.normal(ks[0], (B, S, H), dtype=jnp.float32), 'Wp1': w(ks[1], (H, NAV), H), 'bp1': jnp.zeros((NAV,), jnp.float32), 'Wp2': w(ks[2], (NAV, E), NAV), 'bp2': jnp.zeros((E,), jnp.float32), 'W1': w(ks[3], (E, H, F), H), 'b1': jnp.zeros((E, F), jnp.float32), 'W2': w(ks[4], (E, F, H), F), 'b2': jnp.zeros((E, H), jnp.float32), 'Wo': w(ks[5], (H, H), H), 'bo': jnp.zeros((H,), jnp.float32)}
    _L0_ffn_in = _L0_ffn_setup()
    _d = {'L0_attn_x': _L0_attn_in['x'], 'L0_attn_x_proj_w': _L0_attn_in['x_proj_w'], 'L0_attn_dt_proj_w': _L0_attn_in['dt_proj_w'], 'L0_attn_dt_proj_b': _L0_attn_in['dt_proj_b'], 'L0_attn_A_log': _L0_attn_in['A_log'], 'L0_attn_D': _L0_attn_in['D'], 'L0_attn_x_proj_b_w': _L0_attn_in['x_proj_b_w'], 'L0_attn_dt_proj_b_w': _L0_attn_in['dt_proj_b_w'], 'L0_attn_dt_proj_b_b': _L0_attn_in['dt_proj_b_b'], 'L0_attn_A_b_log': _L0_attn_in['A_b_log'], 'L0_attn_D_b': _L0_attn_in['D_b'], 'L0_ffn_Wp1': _L0_ffn_in['Wp1'], 'L0_ffn_bp1': _L0_ffn_in['bp1'], 'L0_ffn_Wp2': _L0_ffn_in['Wp2'], 'L0_ffn_bp2': _L0_ffn_in['bp2'], 'L0_ffn_W1': _L0_ffn_in['W1'], 'L0_ffn_b1': _L0_ffn_in['b1'], 'L0_ffn_W2': _L0_ffn_in['W2'], 'L0_ffn_b2': _L0_ffn_in['b2'], 'L0_ffn_Wo': _L0_ffn_in['Wo'], 'L0_ffn_bo': _L0_ffn_in['bo']}
    _x0 = _d['L0_attn_x']
    _d['L0_attn_x'] = jax.random.normal(jax.random.fold_in(jax.random.key(seed), 1), (32, 512, 256), dtype=_x0.dtype)
    del _x0
    return _d

def reference(L0_attn_x, L0_attn_x_proj_w, L0_attn_dt_proj_w, L0_attn_dt_proj_b, L0_attn_A_log, L0_attn_D, L0_attn_x_proj_b_w, L0_attn_dt_proj_b_w, L0_attn_dt_proj_b_b, L0_attn_A_b_log, L0_attn_D_b, L0_ffn_Wp1, L0_ffn_bp1, L0_ffn_Wp2, L0_ffn_bp2, L0_ffn_W1, L0_ffn_b1, L0_ffn_W2, L0_ffn_b2, L0_ffn_Wo, L0_ffn_bo):

    def _L0_attn_ref(x, x_proj_w, dt_proj_w, dt_proj_b, A_log, D, x_proj_b_w, dt_proj_b_w, dt_proj_b_b, A_b_log, D_b):
        import jax, jax.numpy as jnp
        import numpy as np
        D_INNER, D_STATE, DT_RANK = (256, 16, 32)

        def _selective_scan(x, x_proj_w, dt_proj_w, dt_proj_b, A_log, Dp):
            A = -jnp.exp(A_log)
            dbc = jnp.einsum('bld,nd->bln', x, x_proj_w)
            delta, Bm, Cm = jnp.split(dbc, [DT_RANK, DT_RANK + D_STATE], axis=-1)
            delta = jax.nn.softplus(jnp.einsum('blr,dr->bld', delta, dt_proj_w) + dt_proj_b)
            deltaA = jnp.exp(delta[..., None] * A)
            BX = delta[..., None] * Bm[:, :, None, :] * x[..., None]

            def comb(e1, e2):
                a1, b1 = e1
                a2, b2 = e2
                return (a2 * a1, a2 * b1 + b2)
            _, hs = jax.lax.associative_scan(comb, (deltaA, BX), axis=1)
            y = jnp.einsum('blds,bls->bld', hs, Cm)
            return y + Dp * x
        y = _selective_scan(x, x_proj_w, dt_proj_w, dt_proj_b, A_log, D)
        xb = x[:, ::-1]
        yb = _selective_scan(xb, x_proj_b_w, dt_proj_b_w, dt_proj_b_b, A_b_log, D_b)
        return y + yb[:, ::-1]

    def _L0_ffn_ref(hidden_states, Wp1, bp1, Wp2, bp2, W1, b1, W2, b2, Wo, bo):
        import jax, jax.numpy as jnp
        import numpy as np
        B, S, H = (8, 1024, 256)
        NAV = 128
        E = 8
        F = 2 * H
        last = hidden_states[:, -1, :]
        logits = jax.nn.gelu(last @ Wp1 + bp1, approximate=False) @ Wp2 + bp2
        action_probs = jax.nn.softmax(logits, axis=-1)
        sel = jnp.argmax(action_probs, axis=-1)
        w1 = W1[sel]
        w2 = W2[sel]
        h = jax.nn.gelu(jnp.einsum('bsh,bhf->bsf', hidden_states, w1) + b1[sel][:, None, :], approximate=False)
        reasoned = jnp.einsum('bsf,bfh->bsh', h, w2) + b2[sel][:, None, :]
        out = reasoned @ Wo + bo
        return hidden_states + 0.3 * out
    x = L0_attn_x
    xn = _layernorm(x, axis=-1)
    s = _L0_attn_ref(xn, L0_attn_x_proj_w, L0_attn_dt_proj_w, L0_attn_dt_proj_b, L0_attn_A_log, L0_attn_D, L0_attn_x_proj_b_w, L0_attn_dt_proj_b_w, L0_attn_dt_proj_b_b, L0_attn_A_b_log, L0_attn_D_b)
    g = _silu(_L0_ffn_ref(xn, L0_ffn_Wp1, L0_ffn_bp1, L0_ffn_Wp2, L0_ffn_bp2, L0_ffn_W1, L0_ffn_b1, L0_ffn_W2, L0_ffn_b2, L0_ffn_Wo, L0_ffn_bo))
    x = x + s * g
    return x

_drawn_inputs = setup_inputs


def setup_inputs(seed=0):
    import zlib

    import numpy as np

    out = dict(_drawn_inputs(seed))
    spreads = {'L0_attn_D': (1.0, 0.2),
     'L0_attn_D_b': (1.0, 0.2),
     'L0_ffn_bp1': (0.0, 0.1),
     'L0_ffn_bp2': (0.0, 0.1),
     'L0_ffn_b1': (0.0, 0.774),
     'L0_ffn_b2': (0.0, 0.505),
     'L0_ffn_bo': (0.0, 0.496)}
    factors = {'L0_attn_x_proj_w': 8.0,
     'L0_attn_dt_proj_w': 8.0,
     'L0_attn_dt_proj_b': 8.0,
     'L0_attn_A_log': 8.0,
     'L0_attn_x_proj_b_w': 8.0,
     'L0_attn_dt_proj_b_w': 8.0,
     'L0_attn_dt_proj_b_b': 8.0,
     'L0_attn_A_b_log': 8.0}
    for name, (base, spread) in spreads.items():
        noise = np.random.default_rng([zlib.crc32(name.encode()), seed]).standard_normal(out[name].shape)
        drawn = base * np.exp(spread * noise) if base else spread * noise
        out[name] = jnp.asarray(drawn.astype(out[name].dtype))
    for name, factor in factors.items():
        out[name] = (out[name] * factor).astype(out[name].dtype)
    return out
```

```python
import concourse.bass as bass
from concourse import mybir
from contextlib import ExitStack


def mamba_moe_block(nc, x, xw_f, dtw_f, dtb_f, alog_f, d_f, xw_b, dtw_b, dtb_b, alog_b, d_b,
                    wp1, bp1, wp2, bp2, w1, b1, w2, b2, wo, bo, out):
    f32, bf16, u32 = mybir.dt.float32, mybir.dt.bfloat16, mybir.dt.uint32
    ALU, ACT = mybir.AluOpType, mybir.ActivationFunctionType

    NB, T, D = x.shape
    P = 128
    DT = D // P
    C = T // P
    N = alog_f.shape[1]
    R = dtw_f.shape[1]
    NE, _, F = w1.shape
    FT = F // P
    STEPS = 2 * N
    UNITS = 17
    RING = 4
    AHEAD = 3
    EPS = 1e-5

    ctx = ExitStack()
    with ctx:
        def sb(name, shape, dt=f32):
            return ctx.enter_context(nc.sbuf_tensor(name, shape, dt))

        def pb(name):
            return ctx.enter_context(nc.psum_tensor(name, [P, T], f32))

        def sem(name):
            return ctx.enter_context(nc.semaphore(name))

        ident = sb("ident", [P, P])
        sel3a = sb("sel3a", [96, 32])
        sel3 = sb("sel3", [96, 32])
        selector = sb("selector", [96, 32, P], bf16)
        ones_row = sb("ones_row", [1, P])
        eps = sb("eps", [P, 1])
        xw_raw = sb("xw_raw", [P, D])
        dtw_raw = sb("dtw_raw", [P, DT, 2 * R])
        wx_delta = sb("wx_delta", [P, DT, 2 * R])
        wx_bc = sb("wx_bc", [P, 2, DT, 96])
        dtw = sb("dtw", [2 * R, DT, P])
        dtb = sb("dtb", [P, 2, DT])
        alog = sb("alog", [P, 2, DT, N])
        rate = sb("rate", [P, 2, DT, N])
        dskip = sb("dskip", [P, 2, DT])
        dsum = sb("dsum", [P, DT])
        diag_d = sb("diag_d", [P, DT, P])
        wo_sb = sb("wo_sb", [P, DT, D])
        bo_row = sb("bo_row", [1, D])
        xl = sb("xl", [NB, D])
        xl_stats = sb("xl_stats", [NB, 6])
        xl_mv = sb("xl_mv", [NB, 2])
        xl_ln = sb("xl_ln", [NB, 1])
        xl_rs = sb("xl_rs", [NB, 1])
        xl_shift = sb("xl_shift", [NB, 1])
        xnl = sb("xnl", [NB, D])
        xlT = sb("xlT", [P, DT, NB])
        wp1_sb = sb("wp1_sb", [P, DT, P])
        bp1_sb = sb("bp1_sb", [P, 1])
        wp2_sb = sb("wp2_sb", [P, NE])
        bp2_row = sb("bp2_row", [1, NE])
        hA = sb("hA", [P, NB])
        lmax = sb("lmax", [NB, 8])
        lneg = sb("lneg", [NB, 1])
        lexp = sb("lexp", [NB, NE])
        lsum = sb("lsum", [NB, 1])
        lrec = sb("lrec", [NB, 1])
        probs = sb("probs", [NB, NE])
        pmax = sb("pmax", [NB, 8])
        pidx = sb("pidx", [NB, 8], u32)
        expert_row = sb("expert_row", [1, NB], u32)
        xin = sb("xin", [P, C, D])
        stats = sb("stats", [P, C, 6])
        mv = sb("mv", [P, C, 2])
        lnv = sb("lnv", [P, C])
        rs = sb("rs", [P, C])
        shift = sb("shift", [P, C])
        xn = sb("xn", [P, C, D])
        xnT = sb("xnT", [P, DT, T])
        dpr = sb("dpr", [2 * R, T])
        bc3 = sb("bc3", [96, 2, 2, T], bf16)
        rest = sb("rest", [96, 2, T])
        mid = sb("mid", [96, 2, T], bf16)
        ex = sb("ex", [P, 2, DT, T])
        relu = sb("relu", [P, 2, DT, T])
        one_ex = sb("one_ex", [P, 2, DT, T])
        lg = sb("lg", [P, 2, DT, T])
        delta = sb("delta", [P, 2, 2, DT, T])
        dx = sb("dx", [P, 2, 2, DT, T])
        w1_sb = sb("w1_sb", [P, DT, F])
        w2_sb = sb("w2_sb", [P, FT, D])
        b1_sb = sb("b1_sb", [P, FT])
        b2_sb = sb("b2_sb", [P, DT])
        hT = sb("hT", [P, FT, T])
        rT = sb("rT", [P, DT, T])
        zz = sb("zz", [P, C, D])
        gate = sb("gate", [P, C, D])
        b_sb = sb("b_sb", [P, RING, T])
        bx = sb("bx", [P, RING, DT, T])
        hs = sb("hs", [P, 2, DT, T])
        hc = sb("hc", [P, RING, DT, T])
        ysb = sb("ysb", [P, 2, T])
        xres = sb("xres", [P, C, D])
        og = sb("og", [P, C, D])

        decay = [pb("decay0"), pb("decay1")]
        cps = [pb("c0"), pb("c1")]
        bps = pb("b0")
        yps = [pb("y0"), pb("y1")]
        pf = pb("front_bank")

        s_wload, s_rload = sem("weights_loaded"), sem("router_loaded")
        s_ident0, s_ident, s_const, s_sel = (sem(n) for n in ("ident0", "ident_ready", "const_ready", "sel_ready"))
        s_wT, s_wev, s_aexp, s_rate = (sem(n) for n in ("wT_ready", "wT_copied", "a_exp", "rate_ready"))
        s_rv, s_ra, s_rp = sem("router_dve"), sem("router_act"), sem("router_pe")
        s_sel_row = sem("expert_row_ready")
        s_x, s_xr, s_w = sem("x_loaded"), sem("xres_loaded"), sem("expert_loaded")
        s_bn, s_mv, s_ln, s_rs, s_shift = (sem(n) for n in ("bn_done", "mv_done", "ln_done", "rs_done", "shift_done"))
        s_xn, s_xnT = sem("xn_done"), sem("xnT_done")
        s_pf, s_pffree = sem("front_bank_full"), sem("front_bank_free")
        s_dpr, s_hi, s_rest, s_mid, s_lo = (sem(n) for n in ("dpr_done", "hi_done", "rest_done", "mid_done", "lo_done"))
        s_abs, s_relu, s_ex, s_onex, s_lg = (sem(n) for n in ("abs_done", "relu_done", "ex_done", "onex_done", "lg_done"))
        s_corr, s_sum, s_delta, s_dx = (sem(n) for n in ("corr_done", "sum_done", "delta_done", "dx_done"))
        s_gelu, s_r, s_zz, s_gate = (sem(n) for n in ("gelu_done", "r_done", "zz_done", "gate_done"))
        s_bps, s_bsb, s_bx = sem("b_psum"), sem("b_sbuf"), sem("bx_done")
        s_decay, s_scan, s_cps, s_hc, s_red = (sem(n) for n in ("decay_done", "scan_done", "c_psum", "hc_done", "sum_states_done"))
        s_yev, s_y, s_yfree = sem("y_copied"), sem("y_tokens"), sem("y_tokens_free")
        s_passed = sem("wait_passed")
        s_yg, s_out, s_store = sem("yg_done"), sem("out_done"), sem("stored")

        def wait(eng, s, value):
            if not isinstance(value, int) or value > 0:
                eng.wait_ge(s, value)

        def wait_alone(eng, s, value):
            if not isinstance(value, int) or value > 0:
                eng.wait_ge(s, value)
                eng.sem_inc(s_passed, 1)

        def rows(body):
            def run(eng):
                for par in range(2):
                    body(par, par, False)
                if NB > 4:
                    with eng.Fori(1, NB // 2 - 1) as i:
                        for par in range(2):
                            body(i * 2 + par, par, False)
                for par in range(2):
                    body(NB - 2 + par, par, par == 1)
            return run

        x_rows = x.rearrange("b (p c) d -> b p (c d)", c=C)
        out_rows = out.rearrange("b (p c) d -> b p (c d)", c=C)
        w1_v = w1.rearrange("e (k p) f -> e p k f", p=P)
        w2_v = w2.rearrange("e (k p) d -> e p k d", p=P)
        b1_v = b1.rearrange("e (k p) -> e p k", p=P)
        b2_v = b2.rearrange("e (k p) -> e p k", p=P)

        def one(view, row):
            return view[row] if isinstance(row, int) else view[bass.ds(row, 1)].squeeze(0)

        block = ctx.enter_context(nc.Block())

        @block.sync
        def _(sp):
            sp.dma_start(xl[:, :], x[:, T - 1, :]).then_inc(s_rload, 16)
            sp.dma_start(wp1_sb[:, :, :], wp1.rearrange("(k p) n -> p k n", p=P)).then_inc(s_rload, 16)
            sp.dma_start(bp1_sb[:, :], bp1.rearrange("(p a) -> p a", a=1)).then_inc(s_rload, 16)
            sp.dma_start(wp2_sb[:, :], wp2).then_inc(s_rload, 16)
            sp.dma_start(bp2_row[:, :], bp2.rearrange("(a n) -> a n", a=1)).then_inc(s_rload, 16)
            sp.dma_start(xin[:, :, :], x_rows[0].rearrange("p (c d) -> p c d", c=C)).then_inc(s_x, 16)
            for g, w in enumerate((xw_f, xw_b)):
                sp.dma_start(xw_raw[64 * g:64 * g + 64, :], w).then_inc(s_wload, 16)
            for g, w in enumerate((dtw_f, dtw_b)):
                sp.dma_start(dtw_raw[:, :, R * g:R * g + R], w.rearrange("(k p) r -> p k r", p=P)).then_inc(s_wload, 16)
            for g, (bias, al, dd) in enumerate(((dtb_f, alog_f, d_f), (dtb_b, alog_b, d_b))):
                sp.dma_start(dtb[:, g, :], bias.rearrange("(k p) -> p k", p=P), allow_slow_non_contiguous=True).then_inc(s_wload, 16)
                sp.dma_start(alog[:, g, :, :], al.rearrange("(k p) n -> p k n", p=P)).then_inc(s_wload, 16)
                sp.dma_start(dskip[:, g, :], dd.rearrange("(k p) -> p k", p=P), allow_slow_non_contiguous=True).then_inc(s_wload, 16)
            sp.dma_start(wo_sb[:, :, :], wo.rearrange("(k p) n -> p k n", p=P)).then_inc(s_wload, 16)
            sp.dma_start(bo_row[:, :], bo.rearrange("(a n) -> a n", a=1)).then_inc(s_wload, 16)

            sp.wait_ge(s_rv, 10)
            sp.dma_start(expert_row[:, :], pidx[:, 0:1], allow_slow_non_contiguous=True).then_inc(s_sel_row, 16)
            sp.wait_ge(s_sel_row, 16)

            def load_expert(row):
                wait_alone(sp, s_r, row * 2)
                sel = sp.value_load(expert_row[0:1, row:row + 1] if isinstance(row, int) else expert_row[0:1, bass.ds(row, 1)],
                                    min_val=0, max_val=NE - 1)
                sp.dma_start(w1_sb[:, :, :], one(w1_v, sel)).then_inc(s_w, 16)
                sp.dma_start(w2_sb[:, :, :], one(w2_v, sel)).then_inc(s_w, 16)
                sp.dma_start(b1_sb[:, :], one(b1_v, sel), allow_slow_non_contiguous=True).then_inc(s_w, 16)
                sp.dma_start(b2_sb[:, :], one(b2_v, sel), allow_slow_non_contiguous=True).then_inc(s_w, 16)

            def load_x(row):
                wait_alone(sp, s_xn, row * C)
                sp.dma_start(xin[:, :, :].rearrange("p c d -> p (c d)"), one(x_rows, row)).then_inc(s_x, 16)

            def store(row):
                wait_alone(sp, s_out, row + 1)
                sp.dma_start(one(out_rows, row), og[:, :, :].rearrange("p c d -> p (c d)")).then_inc(s_store, 16)

            def load_residual(row):
                wait_alone(sp, s_out, row)
                sp.dma_start(xres[:, :, :].rearrange("p c d -> p (c d)"), one(x_rows, row)).then_inc(s_xr, 16)

            load_expert(0)

            def body(row, par, last):
                if not last:
                    load_x(row + 1)
                    load_expert(row + 1)
                if isinstance(row, int) and row == 0:
                    load_residual(row)
                else:
                    store(row - 1)
                    load_residual(row)
            rows(body)(sp)
            store(NB - 1)
            sp.wait_ge(s_store, 16 * NB)

        @block.gpsimd
        def _(pool):
            nc.gpsimd.memset(ident[:, :], 0.0).then_inc(s_ident0, 1)
            nc.gpsimd.memset(ones_row[:, :], 1.0).then_inc(s_const, 1)
            nc.gpsimd.memset(eps[:, :], EPS).then_inc(s_const, 1)
            pool.wait_ge(s_ident0, 1)
            nc.gpsimd.affine_select(out=ident[:, :], in_=ident[:, :], compare_op=ALU.not_equal, fill=1.0, base=0,
                                    pattern=[[-1, P]], channel_multiplier=1).then_inc(s_ident, 1)

            def step_x(row, par, g):
                pool.wait_ge(s_delta, row * 2 + g + 1)
                pool.wait_ge(s_xnT, row * 2 + 2)
                wait(pool, s_bx, (row - 1) * STEPS)
                nc.gpsimd.tensor_tensor(dx[:, par, g, :, :], delta[:, par, g, :, :], xnT[:, :, :], ALU.mult).then_inc(s_dx, 1)

            def times_b(row, par, s):
                g = s // N
                pool.wait_ge(s_bsb, row * STEPS + s + 1)
                if s % N == 0:
                    pool.wait_ge(s_dx, row * 2 + g + 1)
                wait(pool, s_scan, row * 2 * STEPS + 2 * (s - RING) + 2)
                nc.gpsimd.tensor_tensor(bx[:, s % RING, :, :], dx[:, par, g, :, :],
                                        b_sb[:, s % RING, :].unsqueeze(1).broadcast_to([P, DT, T]),
                                        ALU.mult).then_inc(s_bx, 1)

            for g in range(2):
                step_x(0, 0, g)

            def body(row, par, last):
                for s in range(STEPS):
                    times_b(row, par, s)
                    if not last and s in (22, 26):
                        step_x(row + 1, 1 - par, (s - 22) // 4)
            rows(body)(pool)

        @block.scalar
        def _(act):
            A = nc.scalar.activation
            act.wait_ge(s_wload, 12 * 16)
            A(rate[:, :, :, :].rearrange("p a k n -> p (a k n)"), alog[:, :, :, :].rearrange("p a k n -> p (a k n)"),
              ACT.Exp).then_inc(s_aexp, 1)
            act.wait_ge(s_const, 2)
            act.wait_ge(s_rv, 2)
            A(xl_ln[:, :], xl_mv[:, 1:2], ACT.Ln, bias=eps[0:NB, :]).then_inc(s_ra, 1)
            act.wait_ge(s_ra, 1)
            A(xl_rs[:, :], xl_ln[:, :], ACT.Exp, scale=-0.5).then_inc(s_ra, 1)
            act.wait_ge(s_rv, 3)
            A(xnl[:, :], xl[:, :], ACT.Identity, scale=xl_rs[:, :], bias=xl_shift[:, :]).then_inc(s_ra, 1)
            act.wait_ge(s_rp, 2)
            A(hA[:, :], pf[:, 256:256 + NB], ACT.Gelu, bias=bp1_sb[:, :]).then_inc(s_ra, 1)
            act.wait_ge(s_rv, 6)
            A(lexp[:, :], pf[0:NB, 384:384 + NE], ACT.Exp, bias=lneg[:, :], accum_out=lsum[:, :]).then_inc(s_ra, 1)

            def normalise_scale(row):
                act.wait_ge(s_mv, row * C + C)
                wait(act, s_shift, row)
                A(lnv[:, :], mv[:, :, 1], ACT.Ln, bias=eps[:, :]).then_inc(s_ln, 1)
                act.wait_ge(s_ln, row + 1)
                A(rs[:, :], lnv[:, :], ACT.Exp, scale=-0.5).then_inc(s_rs, 1)

            def normalise(row):
                act.wait_ge(s_shift, row + 1)
                wait(act, s_zz, row * 2)
                for c in range(C):
                    A(xn[:, c, :], xin[:, c, :], ACT.Identity, scale=rs[:, c:c + 1], bias=shift[:, c:c + 1]).then_inc(s_xn, 1)

            def copy_xnT(row, k):
                act.wait_ge(s_pf, row * UNITS + k + 1)
                if k == 0:
                    wait(act, s_red, (row - 1) * STEPS + 1)
                    wait(act, s_dx, row * 2)
                A(xnT[:, k, :].rearrange("p (q c) -> p c q", c=C), pf[:, :].rearrange("p (c q) -> p c q", c=C),
                  ACT.Copy).then_inc(s_xnT, 1)
                act.wait_ge(s_xnT, row * 2 + k + 1)
                act.sem_inc(s_pffree, 1)

            def copy_delta_low(row):
                act.wait_ge(s_pf, row * UNITS + 3)
                A(dpr[:, :], pf[0:2 * R, :], ACT.Copy).then_inc(s_pffree, 1)

            def high_part(row, par, g):
                act.wait_ge(s_pf, row * UNITS + 4 + g)
                wait(act, s_bps, (row - 1) * STEPS)
                A(bc3[:, par, g, :], pf[0:96, :], ACT.Copy).then_inc(s_hi, 1)

            def middle_part(row, par, g):
                act.wait_ge(s_rest, row * 2 + g + 1)
                A(bc3[32:64, par, g, :], rest[32:64, g, :], ACT.Copy).then_inc(s_mid, 1)
                wait(act, s_lo, row * 2 - 1 + g)
                A(mid[64:96, g, :], rest[64:96, g, :], ACT.Copy).then_inc(s_mid, 1)

            def absolute(row, q):
                g, k = q // DT, q % DT
                act.wait_ge(s_pf, row * UNITS + 6 + q)
                wait(act, s_corr, (row - 1) * 2 + g + 1)
                A(ex[:, g, k, :], pf[:, :], ACT.Abs, bias=dtb[:, g, k:k + 1]).then_inc(s_abs, 1)
                wait(act, s_delta, (row - 1) * 2 + g + 1)
                A(relu[:, g, k, :], pf[:, :], ACT.Relu, bias=dtb[:, g, k:k + 1]).then_inc(s_pffree, 1)

            def exp_abs(row, g):
                act.wait_ge(s_abs, row * 4 + 2 * g + 2)
                A(ex[:, g, :, :], ex[:, g, :, :], ACT.Exp, scale=-1.0).then_inc(s_ex, 1)

            def one_plus(row, g):
                act.wait_ge(s_ex, row * 2 + g + 1)
                wait(act, s_sum, (row - 1) * 2 + g + 1)
                A(one_ex[:, g, :, :], ex[:, g, :, :], ACT.Copy, bias=1.0).then_inc(s_onex, 1)

            def log_one_plus(row, g):
                wait(act, s_delta, (row - 1) * 2 + g + 1)
                act.wait_ge(s_onex, row * 2 + g + 1)
                A(lg[:, g, :, :], one_ex[:, g, :, :], ACT.Ln).then_inc(s_lg, 1)

            def hidden(row, j):
                act.wait_ge(s_pf, row * UNITS + 10 + j)
                if j == 0:
                    act.wait_ge(s_w, row * 64 + 64)
                A(hT[:, j, :], pf[:, :], ACT.Identity, bias=b1_sb[:, j:j + 1]).then_inc(s_pffree, 1)

            def gelu(row):
                act.wait_ge(s_pffree, row * UNITS + 13)
                A(hT[:, :, :], hT[:, :, :], ACT.Gelu).then_inc(s_gelu, 1)

            def reasoned(row, k):
                act.wait_ge(s_pf, row * UNITS + 14 + k)
                A(rT[:, k, :], pf[:, :], ACT.Identity, bias=b2_sb[:, k:k + 1]).then_inc(s_r, 1)
                act.wait_ge(s_r, row * 2 + k + 1)
                act.sem_inc(s_pffree, 1)

            def silu(row):
                act.wait_ge(s_zz, row * 2 + 2)
                wait(act, s_yg, row * 2)
                A(gate[:, :, :], zz[:, :, :], ACT.Silu).then_inc(s_gate, 1)

            def front(row, par, s):
                if s == 1:
                    normalise_scale(row)
                if s == 2:
                    normalise(row)
                if s in (4, 5):
                    copy_xnT(row, s - 4)
                if s == 7:
                    copy_delta_low(row)
                if s in (8, 10):
                    high_part(row, par, (s - 8) // 2)
                if s in (9, 11):
                    middle_part(row, par, (s - 9) // 2)
                if s in (12, 13, 14, 15):
                    absolute(row, s - 12)
                if s in (14, 17):
                    exp_abs(row, (s - 14) // 3)
                if s in (15, 18):
                    one_plus(row, (s - 15) // 3)
                if s in (16, 19):
                    log_one_plus(row, (s - 16) // 3)
                if s in (18, 19, 20, 21):
                    hidden(row, s - 18)
                if s == 22:
                    gelu(row)
                if s in (25, 26):
                    reasoned(row, s - 25)

            def copy_b(row, s):
                act.wait_ge(s_bps, row * STEPS + s + 1)
                wait(act, s_bx, row * STEPS + s - RING + 1)
                A(b_sb[:, s % RING, :], bps[:, :], ACT.Copy).then_inc(s_bsb, 1)

            def copy_y(row):
                act.wait_ge(s_red, row * STEPS + STEPS)
                wait(act, s_y, row * 2)
                for k in range(2):
                    A(ysb[:, k, :], yps[k][:, :], ACT.Copy).then_inc(s_yev, 1)

            for s in range(STEPS):
                front(0, 0, s)
            for s in range(AHEAD - 1):
                copy_b(0, s)

            def body(row, par, last):
                for s in range(STEPS):
                    g, n = s // N, s % N
                    for k in range(DT):
                        if n == 0:
                            act.wait_ge(s_delta, row * 2 + g + 1)
                        wait(act, s_scan, row * 2 * STEPS + 2 * (s - 1) + k + 1)
                        A(decay[k][:, :], delta[:, par, g, k, :], ACT.Exp, scale=rate[:, g, k, n:n + 1]).then_inc(s_decay, 1)
                    if s == 1 and not (isinstance(row, int) and row == 0):
                        copy_y(row - 1)
                    if s + AHEAD - 1 < STEPS:
                        copy_b(row, s + AHEAD - 1)
                    elif not last:
                        copy_b(row + 1, s + AHEAD - 1 - STEPS)
                    if not last:
                        front(row + 1, 1 - par, s)
                    if s == 22:
                        silu(row)
            act.wait_ge(s_rate, 1)
            rows(body)(act)
            copy_y(NB - 1)

        @block.vector
        def _(dve):
            V = nc.vector
            dve.wait_ge(s_ident, 1)
            V.tensor_tensor(sel3a[:, :], ident[0:96, 0:32], ident[0:96, 32:64], ALU.add).then_inc(s_sel, 1)
            dve.wait_ge(s_sel, 1)
            V.tensor_tensor(sel3[:, :], sel3a[:, :], ident[0:96, 64:96], ALU.add).then_inc(s_sel, 1)
            dve.wait_ge(s_sel, 2)
            V.tensor_copy(selector[:, :, :], sel3[:, :].unsqueeze(2).broadcast_to([96, 32, P])).then_inc(s_sel, 1)
            dve.wait_ge(s_rload, 5 * 16)
            V.bn_stats(xl_stats[:, :], xl[:, :]).then_inc(s_rv, 1)
            dve.wait_ge(s_rv, 1)
            V.bn_aggr(xl_mv[:, :], xl_stats[:, :]).then_inc(s_rv, 1)
            dve.wait_ge(s_ra, 2)
            V.scalar_tensor_tensor(xl_shift[:, :], xl_mv[:, 0:1], -1.0, xl_rs[:, :], ALU.mult, ALU.mult).then_inc(s_rv, 1)
            dve.wait_ge(s_rp, 1)
            V.tensor_copy(xlT[:, :, :], pf[:, 0:DT * NB].rearrange("p (k b) -> p k b", k=DT)).then_inc(s_rv, 1)
            dve.wait_ge(s_rp, 3)
            V.max(lmax[:, :], pf[0:NB, 384:384 + NE]).then_inc(s_rv, 1)
            dve.wait_ge(s_rv, 5)
            V.tensor_scalar(lneg[:, :], lmax[:, 0:1], -1.0, None, ALU.mult).then_inc(s_rv, 1)
            dve.wait_ge(s_ra, 5)
            V.reciprocal(lrec[:, :], lsum[:, :]).then_inc(s_rv, 1)
            dve.wait_ge(s_rv, 7)
            V.tensor_scalar(probs[:, :], lexp[:, :], lrec[:, 0:1], None, ALU.mult).then_inc(s_rv, 1)
            dve.wait_ge(s_rv, 8)
            V.max(pmax[:, :], probs[:, :]).then_inc(s_rv, 1)
            dve.wait_ge(s_rv, 9)
            V.max_index(pidx[:, :], pmax[:, :], probs[:, :]).then_inc(s_rv, 1)
            dve.wait_ge(s_wT, 1)
            wT = pf[:, 0:2 * P].rearrange("p (k g m) -> p k g m", k=DT, g=2)
            for g in range(2):
                V.tensor_copy(wx_delta[:, :, R * g:R * g + R], wT[:, :, g, 0:R]).then_inc(s_wev, 1)
                for k in range(DT):
                    V.tensor_copy(wx_bc[:, g, k, :].rearrange("p (a m) -> p a m", a=3),
                                  wT[:, k, g, R:64].unsqueeze(1).broadcast_to([P, 3, 32])).then_inc(s_wev, 1)
            V.tensor_copy(dtw[:, :, :], pf[0:2 * R, 2 * P:4 * P].rearrange("r (k m) -> r k m", k=DT)).then_inc(s_wev, 1)
            V.tensor_tensor(dsum[:, :], dskip[:, 0, :], dskip[:, 1, :], ALU.add).then_inc(s_wev, 1)
            dve.wait_ge(s_wev, 8)
            for k in range(DT):
                V.tensor_scalar(diag_d[:, k, :], ident[:, :], dsum[:, k:k + 1], None, ALU.mult).then_inc(s_wev, 1)
            dve.wait_ge(s_aexp, 1)
            V.tensor_scalar(rate[:, :, :, :].rearrange("p a k n -> p (a k n)"), rate[:, :, :, :].rearrange("p a k n -> p (a k n)"),
                            -1.0, None, ALU.mult).then_inc(s_rate, 1)

            def mean_variance(row):
                dve.wait_ge(s_x, row * 16 + 16)
                wait(dve, s_shift, row)
                for c in range(C):
                    V.bn_stats(stats[:, c, :], xin[:, c, :]).then_inc(s_bn, 1)
                wait_alone(dve, s_bn, row * C + C)
                for c in range(C):
                    V.bn_aggr(mv[:, c, :], stats[:, c, :]).then_inc(s_mv, 1)

            def shift_of(row):
                dve.wait_ge(s_rs, row + 1)
                wait(dve, s_xn, row * C)
                V.scalar_tensor_tensor(shift[:, :], mv[:, :, 0], -1.0, rs[:, :], ALU.mult, ALU.mult).then_inc(s_shift, 1)

            def rest_of(row, par, g):
                dve.wait_ge(s_hi, row * 2 + g + 1)
                wait(dve, s_lo, (row - 1) * 2 + g + 1)
                V.tensor_tensor(rest[:, g, :], pf[0:96, :], bc3[:, par, g, :], ALU.subtract).then_inc(s_rest, 1)
                dve.wait_ge(s_rest, row * 2 + g + 1)
                dve.sem_inc(s_pffree, 1)

            def low_part(row, par, g):
                dve.wait_ge(s_mid, row * 4 + 2 * g + 2)
                V.tensor_tensor(bc3[64:96, par, g, :], rest[64:96, g, :], mid[64:96, g, :],
                                ALU.subtract).then_inc(s_lo, 1)

            def correction(row, g):
                dve.wait_ge(s_lg, row * 2 + g + 1)
                V.scalar_tensor_tensor(one_ex[:, g, :, :], one_ex[:, g, :, :], 1.0, ex[:, g, :, :],
                                       ALU.subtract, ALU.subtract).then_inc(s_corr, 1)

            def log1p(row, g):
                dve.wait_ge(s_corr, row * 2 + g + 1)
                V.tensor_tensor(lg[:, g, :, :], lg[:, g, :, :], one_ex[:, g, :, :], ALU.subtract).then_inc(s_sum, 1)

            def step_size(row, par, g):
                dve.wait_ge(s_sum, row * 2 + g + 1)
                dve.wait_ge(s_pffree, row * UNITS + 7 + 2 * g)
                wait(dve, s_decay, (row - 1) * 2 * STEPS)
                V.tensor_tensor(delta[:, par, g, :, :], lg[:, g, :, :], relu[:, g, :, :], ALU.add).then_inc(s_delta, 1)

            def gate_input(row, v):
                dve.wait_ge(s_pf, row * UNITS + 16 + v)
                if v == 0:
                    wait(dve, s_gate, row)
                V.scalar_tensor_tensor(zz[:, 2 * v:2 * v + 2, :], pf[:, :].rearrange("p (c d) -> p c d", c=2), 0.3,
                                       xn[:, 2 * v:2 * v + 2, :], ALU.mult, ALU.add).then_inc(s_zz, 1)
                dve.wait_ge(s_zz, row * 2 + v + 1)
                dve.sem_inc(s_pffree, 1)

            def front(row, par, s):
                if s == 0:
                    mean_variance(row)
                if s == 1:
                    shift_of(row)
                if s in (8, 10):
                    rest_of(row, par, (s - 8) // 2)
                if s in (10, 12):
                    low_part(row, par, (s - 10) // 2)
                if s == 17:
                    correction(row, 0)
                if s == 18:
                    log1p(row, 0)
                if s == 19:
                    step_size(row, par, 0)
                if s == 22:
                    correction(row, 1)
                    log1p(row, 1)
                    step_size(row, par, 1)
                if s in (28, 29):
                    gate_input(row, s - 28)

            def output(row, par, v):
                dve.wait_ge(s_y, row * 2 + v + 1)
                dve.wait_ge(s_gate, row + 1)
                wait(dve, s_store, row * 16)
                V.tensor_tensor(og[:, 2 * v:2 * v + 2, :], yps_tok(v), gate[:, 2 * v:2 * v + 2, :], ALU.mult).then_inc(s_yg, 1)
                dve.wait_ge(s_yg, row * 2 + v + 1)
                dve.sem_inc(s_yfree, 1)

            def yps_tok(v):
                return pf[:, :].rearrange("p (c d) -> p c d", c=2)

            def residual(row):
                dve.wait_ge(s_yg, row * 2 + 2)
                dve.wait_ge(s_xr, row * 16 + 16)
                V.tensor_tensor(og[:, :, :], og[:, :, :], xres[:, :, :], ALU.add).then_inc(s_out, 1)

            def times_c(row, s):
                dve.wait_ge(s_scan, row * 2 * STEPS + 2 * s + 2)
                dve.wait_ge(s_cps, row * STEPS + s + 1)
                wait(dve, s_red, row * STEPS + s - RING + 1)
                V.tensor_tensor(hc[:, s % RING, :, :], hs[:, s % 2, :, :],
                                cps[s % 2][:, :].unsqueeze(1).broadcast_to([P, DT, T]), ALU.mult).then_inc(s_hc, 1)

            def scan(row, s, k):
                g = s // N
                u = slice(None) if g == 0 else slice(None, None, -1)
                dve.wait_ge(s_bx, row * STEPS + s + 1)
                dve.wait_ge(s_decay, row * 2 * STEPS + 2 * s + k + 1)
                wait(dve, s_hc, row * STEPS + s - 1)
                V.tensor_tensor_scan(hs[:, s % 2, k, u], decay[k][:, u], bx[:, s % RING, k, u], 0.0,
                                     ALU.mult, ALU.add).then_inc(s_scan, 1)

            for s in range(STEPS):
                front(0, 0, s)

            def body(row, par, last):
                for s in range(STEPS):
                    scan(row, s, 0)
                    if s:
                        times_c(row, s - 1)
                    scan(row, s, 1)
                    if not (isinstance(row, int) and row == 0):
                        if s in (3, 4):
                            output(row - 1, 1 - par, s - 3)
                        if s == 5:
                            residual(row - 1)
                    if not last:
                        front(row + 1, 1 - par, s)
                times_c(row, STEPS - 1)
            rows(body)(dve)
            for v in range(2):
                output(NB - 1, 1, v)
            residual(NB - 1)

        @block.tensor
        def _(pe):
            M = nc.tensor.matmul
            pe.wait_ge(s_ident, 1)
            pe.wait_ge(s_ra, 3)
            for k in range(DT):
                ins = nc.tensor.transpose(pf[:, k * NB:(k + 1) * NB], xnl[:, k * P:(k + 1) * P], ident[0:NB, 0:NB])
            ins.then_inc(s_rp, 1)
            pe.wait_ge(s_rv, 4)
            for k in range(DT):
                ins = M(pf[:, 256:256 + NB], wp1_sb[:, k, :], xlT[:, k, :], start=(k == 0), stop=(k == DT - 1))
            ins.then_inc(s_rp, 1)
            pe.wait_ge(s_ra, 4)
            M(pf[0:NB, 384:384 + NE], hA[:, :], wp2_sb[:, :], start=True, stop=False)
            M(pf[0:NB, 384:384 + NE], ones_row[:, 0:NB], bp2_row[:, :], start=False, stop=True).then_inc(s_rp, 1)
            pe.wait_ge(s_wload, 12 * 16)
            pe.wait_ge(s_ra, 5)
            for k in range(DT):
                nc.tensor.transpose(pf[:, k * P:(k + 1) * P], xw_raw[:, k * P:(k + 1) * P], ident[:, :])
            for k in range(DT):
                ins = nc.tensor.transpose(pf[0:2 * R, (2 + k) * P:(3 + k) * P], dtw_raw[:, k, :], ident[:, :])
            ins.then_inc(s_wT, 1)
            pe.wait_ge(s_wev, 10)
            pe.wait_ge(s_sel, 3)

            def unit(row, u):
                wait(pe, s_pffree, row * UNITS + u)
                if u == 0:
                    wait(pe, s_yfree, (row - 1) * 2)

            def transpose_xn(row, k):
                unit(row, k)
                for c in range(C):
                    pe.wait_ge(s_xn, row * C + C)
                    ins = nc.tensor.transpose(pf[:, c * P:(c + 1) * P], xn[:, c, k * P:(k + 1) * P], ident[:, :])
                ins.then_inc(s_pf, 1)

            def project_delta(row):
                unit(row, 2)
                pe.wait_ge(s_xnT, row * 2 + 2)
                for k in range(DT):
                    ins = M(pf[0:2 * R, :], wx_delta[:, k, :], xnT[:, k, :], start=(k == 0), stop=(k == DT - 1))
                ins.then_inc(s_pf, 1)

            def project_bc(row, g):
                unit(row, 3 + g)
                for k in range(DT):
                    ins = M(pf[0:96, :], wx_bc[:, g, k, :], xnT[:, k, :], start=(k == 0), stop=(k == DT - 1))
                ins.then_inc(s_pf, 1)

            def expand_delta(row, q):
                g, k = q // DT, q % DT
                unit(row, 5 + q)
                M(pf[:, :], dtw[R * g:R * g + R, k, :], dpr[R * g:R * g + R, :], start=True, stop=True).then_inc(s_pf, 1)

            def ffn_in(row, j):
                unit(row, 9 + j)
                pe.wait_ge(s_w, row * 64 + 64)
                for k in range(DT):
                    ins = M(pf[:, :], w1_sb[:, k, j * P:(j + 1) * P], xnT[:, k, :], start=(k == 0), stop=(k == DT - 1))
                ins.then_inc(s_pf, 1)

            def ffn_out(row, m):
                unit(row, 13 + m)
                pe.wait_ge(s_gelu, row + 1)
                for j in range(FT):
                    ins = M(pf[:, :], w2_sb[:, j, m * P:(m + 1) * P], hT[:, j, :], start=(j == 0), stop=(j == FT - 1))
                ins.then_inc(s_pf, 1)

            def ffn_final(row, v):
                unit(row, 15 + v)
                for h in range(2):
                    c, to = 2 * v + h, pf[:, h * D:(h + 1) * D]
                    for k in range(DT):
                        M(to, rT[:, k, :].rearrange("p (q c) -> p c q", c=C)[:, c, :], wo_sb[:, k, :], start=(k == 0), stop=False)
                    ins = M(to, ones_row[:, :], bo_row[:, :], start=False, stop=True)
                ins.then_inc(s_pf, 1)

            def front(row, s):
                if s in (3, 4):
                    transpose_xn(row, s - 3)
                if s == 6:
                    project_delta(row)
                if s in (7, 9):
                    project_bc(row, (s - 7) // 2)
                if s in (11, 12, 13, 14):
                    expand_delta(row, s - 11)
                if s in (17, 18, 19, 20):
                    ffn_in(row, s - 17)
                if s in (24, 25):
                    ffn_out(row, s - 24)
                if s in (27, 28):
                    ffn_final(row, s - 27)

            def broadcast_b(row, par, s):
                wait(pe, s_bsb, row * STEPS + s)
                if s == 0:
                    pe.wait_ge(s_lo, row * 2 + 2)
                g, n = s // N, s % N
                M(bps[:, :], selector[:, n, :], bc3[:, par, g, :], start=True, stop=True).then_inc(s_bps, 1)

            def broadcast_c(row, par, s):
                wait(pe, s_hc, row * STEPS + s - 1)
                g, n = s // N, s % N
                M(cps[s % 2][:, :], selector[:, N + n, :], bc3[:, par, g, :], start=True, stop=True).then_inc(s_cps, 1)

            def skip_term(row):
                wait(pe, s_yev, row * 2)
                for k in range(DT):
                    M(yps[k][:, :], diag_d[:, k, :], xnT[:, k, :], start=True, stop=False)

            def add_state(row, s):
                pe.wait_ge(s_hc, row * STEPS + s + 1)
                for k in range(DT):
                    ins = M(yps[k][:, :], ident[:, :], hc[:, s % RING, k, :], start=False, stop=(s == STEPS - 1))
                ins.then_inc(s_red, 1)

            def tokens_of_y(row, v):
                wait(pe, s_yfree, row * 2 + v)
                pe.wait_ge(s_pffree, (row + 2) * UNITS) if not (isinstance(row, int) and row == NB - 1) else pe.wait_ge(s_pffree, NB * UNITS)
                pe.wait_ge(s_yev, row * 2 + 2)
                for h in range(2):
                    for k in range(DT):
                        to = pf[:, h * D + k * P:h * D + (k + 1) * P]
                        ins = nc.tensor.transpose(to, ysb[:, k, :].rearrange("p (q c) -> p c q", c=C)[:, 2 * v + h, :], ident[:, :])
                ins.then_inc(s_y, 1)

            for s in range(STEPS):
                front(0, s)
            for s in range(AHEAD):
                broadcast_b(0, 0, s)
            broadcast_c(0, 0, 0)

            def body(row, par, last):
                for s in range(STEPS):
                    if s + 1 < STEPS:
                        broadcast_c(row, par, s + 1)
                    elif not last:
                        broadcast_c(row + 1, 1 - par, 0)
                    if s + AHEAD < STEPS:
                        broadcast_b(row, par, s + AHEAD)
                    elif not last:
                        broadcast_b(row + 1, 1 - par, s + AHEAD - STEPS)
                    if s in (1, 2) and not (isinstance(row, int) and row == 0):
                        tokens_of_y(row - 1, s - 1)
                    if not last:
                        front(row + 1, s)
                    if s == 0:
                        skip_term(row)
                    add_state(row, s)
            rows(body)(pe)
            for v in range(2):
                tokens_of_y(NB - 1, v)


_INS = ["L0_attn_x", "L0_attn_x_proj_w", "L0_attn_dt_proj_w", "L0_attn_dt_proj_b", "L0_attn_A_log", "L0_attn_D",
        "L0_attn_x_proj_b_w", "L0_attn_dt_proj_b_w", "L0_attn_dt_proj_b_b", "L0_attn_A_b_log", "L0_attn_D_b",
        "L0_ffn_Wp1", "L0_ffn_bp1", "L0_ffn_Wp2", "L0_ffn_bp2", "L0_ffn_W1", "L0_ffn_b1", "L0_ffn_W2", "L0_ffn_b2",
        "L0_ffn_Wo", "L0_ffn_bo"]


def kernel(**inputs):
    import numpy as _np
    import concourse.bacc as _bacc
    from concourse.bass_utils import run_bass_kernel_spmd as _run

    nc = _bacc.Bacc("TRN2", target_bir_lowering=False, num_devices=1)
    arrays, args = {}, []
    for name in _INS:
        a = _np.ascontiguousarray(inputs[name])
        arrays[f"in_{name}_dram"] = a
        args.append(nc.dram_tensor(f"in_{name}_dram", a.shape, mybir.dt.from_np(a.dtype), kind="ExternalInput").ap())
    out = nc.dram_tensor("out_0_dram", inputs["L0_attn_x"].shape, mybir.dt.float32, kind="ExternalOutput").ap()
    mamba_moe_block(nc, *args, out)
    r = _run(nc, [arrays], core_ids=[0])
    return r.results[0]["out_0_dram"]
```

```python
import concourse.bass as bass
from concourse import mybir
from contextlib import ExitStack


def mamba_moe_block(nc, x, xw_f, dtw_f, dtb_f, alog_f, d_f, xw_b, dtw_b, dtb_b, alog_b, d_b,
                    wp1, bp1, wp2, bp2, w1, b1, w2, b2, wo, bo,
                    w2o_dram, bias_dram, out):
    f32, bf16, u32 = mybir.dt.float32, mybir.dt.bfloat16, mybir.dt.uint32
    ALU, ACT = mybir.AluOpType, mybir.ActivationFunctionType

    NB, T, D = x.shape
    P = 128
    DT = D // P
    C = T // P
    N = alog_f.shape[1]
    R = dtw_f.shape[1]
    NE, _, F = w1.shape
    FT = F // P
    STEPS = 2 * N
    UNITS = 13
    RING = 4
    AHEAD = 4
    LEAD = 3
    EPS = 1e-5
    LN_SLACK = 7e-8
    SQ_SCALE, SQ_SHIFT, SQ_REST = 3 ** -0.5, -(3 ** 0.5) / 4, 13 / 16

    ctx = ExitStack()
    with ctx:
        def sb(name, shape, dt=f32):
            return ctx.enter_context(nc.sbuf_tensor(name, shape, dt))

        def pb(name):
            return ctx.enter_context(nc.psum_tensor(name, [P, T], f32))

        def sem(name):
            return ctx.enter_context(nc.semaphore(name))

        ident = sb("ident", [P, P])
        sel3a = sb("sel3a", [96, 32])
        sel3 = sb("sel3", [96, 32])
        selector = sb("selector", [96, 32, P], bf16)
        ones_row = sb("ones_row", [1, P])
        eps = sb("eps", [P, 1])
        sq_shift = sb("sq_shift", [P, 1])
        xw_raw = sb("xw_raw", [P, D])
        dtw_raw = sb("dtw_raw", [P, DT, P])
        wx = sb("wx", [P, DT, P])
        dtw = sb("dtw", [P, DT, P])
        dtb = sb("dtb", [P, 2, DT])
        alog = sb("alog", [P, 2, DT, N])
        rate = sb("rate", [P, 2, DT, N])
        dskip = sb("dskip", [P, 2, DT])
        dsum = sb("dsum", [P, DT])
        diag_d = sb("diag_d", [P, DT, P])
        wo_sb = sb("wo_sb", [P, DT, D])
        bo_row = sb("bo_row", [1, D])
        b2T = sb("b2T", [P, DT, NE])
        bias_rest = sb("bias_rest", [NE, D])
        bias_rest2 = sb("bias_rest2", [NE, D])
        bias_part = sb("bias_part", [NE, 3, D], bf16)
        ones3 = sb("ones3", [3, P], bf16)
        xl = sb("xl", [NB, D])
        xl_stats = sb("xl_stats", [NB, 6])
        xl_mv = sb("xl_mv", [NB, 2])
        xl_ln = sb("xl_ln", [NB, 1])
        xl_rs = sb("xl_rs", [NB, 1])
        xl_nwt = sb("xl_nwt", [NB, 2])
        xl_shift = sb("xl_shift", [NB, 1])
        xnl = sb("xnl", [NB, D])
        xlT = sb("xlT", [P, DT, NB])
        wp1_sb = sb("wp1_sb", [P, DT, P])
        bp1_sb = sb("bp1_sb", [P, 1])
        wp2_sb = sb("wp2_sb", [P, NE])
        bp2_row = sb("bp2_row", [1, NE])
        hA = sb("hA", [P, NB])
        lmax = sb("lmax", [NB, 8])
        lneg = sb("lneg", [NB, 1])
        lexp = sb("lexp", [NB, NE])
        lsum = sb("lsum", [NB, 1])
        lrec = sb("lrec", [NB, 1])
        probs = sb("probs", [NB, NE])
        pmax = sb("pmax", [NB, 8])
        pidx = sb("pidx", [NB, 8], u32)
        expert_row = sb("expert_row", [1, NB], u32)
        xin = sb("xin", [P, C, D])
        stats = sb("stats", [P, C, 6])
        mv = sb("mv", [P, C, 2])
        lnv = sb("lnv", [P, C])
        rs = sb("rs", [P, C])
        nwt = sb("nwt", [P, 2, C])
        shift = sb("shift", [P, C])
        xn = sb("xn", [P, C, D])
        xnT = sb("xnT", [P, DT, T])
        dpr = sb("dpr", [P, T])
        high = sb("high", [P, T], bf16)
        bc3 = sb("bc3", [96, 2, 2, T], bf16)
        rest = sb("rest", [P, T])
        mid = sb("mid", [P, T], bf16)
        low = sb("low", [P, T], bf16)
        ex = sb("ex", [P, 2, DT, T])
        poly = sb("poly", [P, 2, DT, T])
        lg = sb("lg", [P, 2, DT, T])
        delta = sb("delta", [P, 2, 2, DT, T])
        dx = sb("dx", [P, 2, 2, DT, T])
        w1_sb = sb("w1_sb", [P, DT, F])
        w2o_sb = sb("w2o_sb", [P, FT, D])
        b1_sb = sb("b1_sb", [P, FT])
        bias3 = sb("bias3", [3, D], bf16)
        hT = sb("hT", [P, FT, T])
        zz = sb("zz", [P, C, D])
        gate = sb("gate", [P, C, D])
        b_sb = sb("b_sb", [P, RING, T])
        decay = sb("decay", [P, RING, DT, T])
        bx = sb("bx", [P, RING, DT, T])
        hs = sb("hs", [P, 2, DT, T])
        hc = sb("hc", [P, RING, DT, T])
        ysb = sb("ysb", [P, 2, T])
        xres = sb("xres", [P, C, D])
        og = sb("og", [P, C, D])
        w2_in = (w2o_sb, xres)
        w2T = ysb[:, :, :].rearrange("p a (j k f) -> p (a j) k f", k=DT, f=P)
        w2o_st = (og, gate)

        cps = [pb("c0"), pb("c1")]
        bps = [pb("b0"), pb("b1")]
        yps = [pb("y0"), pb("y1")]
        fps = [pb("front0"), pb("front1")]
        w2T_ps, w2o_ps = yps, (cps, bps)
        router_ps, weights_ps, bias_ps = cps[1], bps[1], yps[0]

        s_wload, s_rload = sem("weights_loaded"), sem("router_loaded")
        s_ident0, s_ident, s_const, s_sel = (sem(n) for n in ("ident0", "ident_ready", "const_ready", "sel_ready"))
        s_wT, s_wev, s_aexp, s_rate = (sem(n) for n in ("wT_ready", "wT_copied", "a_exp", "rate_ready"))
        s_rv, s_ra, s_rp = sem("router_dve"), sem("router_act"), sem("router_pe")
        s_sel_row = sem("expert_row_ready")
        s_x, s_xr, s_w = sem("x_loaded"), sem("xres_loaded"), sem("expert_loaded")
        s_bn, s_mv, s_ln, s_rs, s_shift = (sem(n) for n in ("bn_done", "mv_done", "ln_done", "rs_done", "shift_done"))
        s_xn, s_xnT = sem("xn_done"), sem("xnT_done")
        s_pf, s_hid = sem("front_bank_full"), sem("hidden_copied")
        s_dpr, s_hi, s_rest, s_mid, s_lo = (sem(n) for n in (
            "dpr_done", "hi_done", "rest_done", "mid_done", "lo_done"))
        s_abs, s_relu, s_ex, s_sq, s_lg = (sem(n) for n in ("abs_done", "relu_done", "ex_done", "square_done", "lg_done"))
        s_poly, s_min, s_delta, s_dx = (sem(n) for n in ("poly_done", "log1p_done", "delta_done", "dx_done"))
        s_gelu, s_zz, s_gate = (sem(n) for n in ("gelu_done", "zz_done", "gate_done"))
        s_bc3, s_quad = sem("bc3_moved"), sem("quadratic_done")
        s_nwt, s_xnwt = sem("newton_steps"), sem("router_newton_steps")
        s_wo = sem("wo_loaded")
        s_w2, s_w2st = (sem("w2_loaded0"), sem("w2_loaded1")), (sem("w2o_stored0"), sem("w2o_stored1"))
        s_w2T, s_w2Tc, s_w2o, s_w2oc = (sem(n) for n in ("w2T_ready", "w2T_copied", "w2o_ready", "w2o_copied"))
        s_bias, s_biasc, s_biasst, s_b2T, s_dtz = (sem(n) for n in ("bias_ready", "bias_parts", "bias_stored", "b2T_loaded", "dtw_zeroed"))
        s_bps, s_bsb, s_bx = sem("b_psum"), sem("b_sbuf"), sem("bx_done")
        s_decay, s_scan, s_cps, s_hc, s_red = (sem(n) for n in ("decay_done", "scan_done", "c_psum", "hc_done", "sum_states_done"))
        s_skip = sem("skip_done")
        s_yev, s_y = sem("y_copied"), sem("y_tokens")
        s_passed = sem("wait_passed")
        s_yg, s_out, s_store = sem("yg_done"), sem("out_done"), sem("stored")

        def wait(eng, s, value):
            if not isinstance(value, int) or value > 0:
                eng.wait_ge(s, value)

        def wait_alone(eng, s, value):
            if not isinstance(value, int) or value > 0:
                eng.wait_ge(s, value)
                eng.sem_inc(s_passed, 1)

        def rows(body):
            def run(eng):
                for par in range(2):
                    body(par, par, False)
                if NB > 4:
                    with eng.Fori(1, NB // 2 - 1) as i:
                        for par in range(2):
                            body(i * 2 + par, par, False)
                for par in range(2):
                    body(NB - 2 + par, par, par == 1)
            return run

        x_rows = x.rearrange("b (p c) d -> b p (c d)", c=C)
        out_rows = out.rearrange("b (p c) d -> b p (c d)", c=C)
        w1_v = w1.rearrange("e (k p) f -> e p k f", p=P)
        w2_v = w2.rearrange("e (k p) d -> e p k d", p=P)
        b1_v = b1.rearrange("e (k p) -> e p k", p=P)
        w2o_v = w2o_dram.rearrange("e (k p) d -> e p k d", p=P)

        def one(view, row):
            return view[row] if isinstance(row, int) else view[bass.ds(row, 1)].squeeze(0)

        block = ctx.enter_context(nc.Block())

        @block.sync
        def _(sp):
            sp.dma_start(wo_sb[:, :, :], wo.rearrange("(k p) n -> p k n", p=P)).then_inc(s_wo, 16)
            for e in range(2):
                sp.dma_start(w2_in[e][:, :, :], w2_v[e]).then_inc(s_w2[e], 16)
            sp.dma_start(xin[:, :, :], x_rows[0].rearrange("p (c d) -> p c d", c=C)).then_inc(s_x, 16)
            sp.dma_start(xl[:, :], x[:, T - 1, :]).then_inc(s_rload, 16)
            sp.dma_start(wp1_sb[:, :, :], wp1.rearrange("(k p) n -> p k n", p=P)).then_inc(s_rload, 16)
            sp.dma_start(bp1_sb[:, :], bp1.rearrange("(p a) -> p a", a=1)).then_inc(s_rload, 16)
            sp.dma_start(wp2_sb[:, :], wp2).then_inc(s_rload, 16)
            sp.dma_start(bp2_row[:, :], bp2.rearrange("(a n) -> a n", a=1)).then_inc(s_rload, 16)
            for g, w in enumerate((xw_f, xw_b)):
                sp.dma_start(xw_raw[64 * g:64 * g + 64, :], w).then_inc(s_wload, 16)
            sp.wait_ge(s_dtz, 1)
            for g, w in enumerate((dtw_f, dtw_b)):
                sp.dma_start(dtw_raw[:, :, 64 * g:64 * g + R], w.rearrange("(k p) r -> p k r", p=P)).then_inc(s_wload, 16)
            for g, (bias, al, dd) in enumerate(((dtb_f, alog_f, d_f), (dtb_b, alog_b, d_b))):
                sp.dma_start(dtb[:, g, :], bias.rearrange("(k p) -> p k", p=P), allow_slow_non_contiguous=True).then_inc(s_wload, 16)
                sp.dma_start(alog[:, g, :, :], al.rearrange("(k p) n -> p k n", p=P)).then_inc(s_wload, 16)
                sp.dma_start(dskip[:, g, :], dd.rearrange("(k p) -> p k", p=P), allow_slow_non_contiguous=True).then_inc(s_wload, 16)
            sp.dma_start(bo_row[:, :], bo.rearrange("(a n) -> a n", a=1)).then_inc(s_wload, 16)

            for k in range(DT):
                sp.dma_start(b2T[:, k, :], b2[:, k * P:(k + 1) * P].rearrange("e p -> p e"),
                             allow_slow_non_contiguous=True).then_inc(s_b2T, 16)

            def store_w2o(i, a):
                wait_alone(sp, s_w2oc, i * 4 + 2 * a + 2)
                sp.dma_start(one(w2o_v, i * 2 - 2 + a), w2o_st[a][:, :, :]).then_inc(s_w2st[a], 16)

            with sp.Fori(1, NE // 2) as i:
                for a in range(2):
                    wait_alone(sp, s_w2T, i * 4 + 2 * a - 2)
                    sp.dma_start(w2_in[a][:, :, :], one(w2_v, i * 2 + a)).then_inc(s_w2[a], 16)
                    store_w2o(i, a)
            for a in range(2):
                store_w2o(NE // 2, a)
            sp.wait_ge(s_biasc, 5)
            sp.dma_start(bias_dram, bias_part[:, :, :]).then_inc(s_biasst, 16)

            sp.wait_ge(s_rv, 10)
            sp.dma_start(expert_row[:, :], pidx[:, 0:1], allow_slow_non_contiguous=True).then_inc(s_sel_row, 16)
            sp.wait_ge(s_biasst, 16)
            for a in range(2):
                sp.wait_ge(s_w2st[a], 16 * (NE // 2 + 1))
            sp.wait_ge(s_sel_row, 16)

            def load_expert(row):
                wait_alone(sp, s_pf, row * UNITS)
                wait_alone(sp, s_gelu, row)
                sel = sp.value_load(expert_row[0:1, row:row + 1] if isinstance(row, int) else expert_row[0:1, bass.ds(row, 1)],
                                    min_val=0, max_val=NE - 1)
                sp.dma_start(w1_sb[:, :, :], one(w1_v, sel)).then_inc(s_w, 16)
                sp.dma_start(w2o_sb[:, :, :], one(w2o_v, sel)).then_inc(s_w, 16)
                sp.dma_start(b1_sb[:, :], one(b1_v, sel), allow_slow_non_contiguous=True).then_inc(s_w, 16)
                sp.dma_start(bias3[:, :], one(bias_dram, sel)).then_inc(s_w, 16)

            def load_x(row):
                wait_alone(sp, s_xn, row * C)
                sp.dma_start(xin[:, :, :].rearrange("p c d -> p (c d)"), one(x_rows, row)).then_inc(s_x, 16)

            def store(row):
                wait_alone(sp, s_out, row + 1)
                sp.dma_start(one(out_rows, row), og[:, :, :].rearrange("p c d -> p (c d)")).then_inc(s_store, 16)

            def load_residual(row):
                wait_alone(sp, s_out, row)
                sp.dma_start(xres[:, :, :].rearrange("p c d -> p (c d)"), one(x_rows, row)).then_inc(s_xr, 16)

            def move_bc(row, par):
                wait_alone(sp, s_bps, (row - 1) * STEPS)
                wait_alone(sp, s_cps, (row - 1) * STEPS)
                wait_alone(sp, s_lo, row + 1)
                for a, part in enumerate((high, mid, low)):
                    for g in range(2):
                        sp.dma_start(bc3[32 * a:32 * a + 32, par, g, :],
                                     part[64 * g + R:64 * g + R + 32, :]).then_inc(s_bc3, 16)

            load_expert(0)
            move_bc(0, 0)

            def body(row, par, last):
                if not last:
                    load_x(row + 1)
                    load_expert(row + 1)
                if isinstance(row, int) and row == 0:
                    load_residual(row)
                else:
                    store(row - 1)
                    load_residual(row)
                if not last:
                    move_bc(row + 1, 1 - par)
            rows(body)(sp)
            store(NB - 1)
            sp.wait_ge(s_store, 16 * NB)

        @block.gpsimd
        def _(pool):
            nc.gpsimd.memset(ident[:, :], 0.0).then_inc(s_ident0, 1)
            nc.gpsimd.memset(ones_row[:, :], 1.0).then_inc(s_const, 1)
            nc.gpsimd.memset(eps[:, :], EPS).then_inc(s_const, 1)
            nc.gpsimd.memset(sq_shift[:, :], SQ_SHIFT).then_inc(s_const, 1)
            nc.gpsimd.memset(ones3[:, :], 1.0).then_inc(s_const, 1)
            nc.gpsimd.memset(dtw_raw[:, :, :], 0.0).then_inc(s_dtz, 1)
            pool.wait_ge(s_ident0, 1)
            nc.gpsimd.affine_select(out=ident[:, :], in_=ident[:, :], compare_op=ALU.not_equal, fill=1.0, base=0,
                                    pattern=[[-1, P]], channel_multiplier=1).then_inc(s_ident, 1)

            def step_x(row, par, g):
                pool.wait_ge(s_delta, row * 2 + g + 1)
                pool.wait_ge(s_xnT, row * 2 + 2)
                wait(pool, s_bx, (row - 1) * STEPS)
                nc.gpsimd.tensor_tensor(dx[:, par, g, :, :], delta[:, par, g, :, :], xnT[:, :, :], ALU.mult).then_inc(s_dx, 1)

            def polynomial(row, g):
                pool.wait_ge(s_quad, row * 2 + g + 1)
                nc.gpsimd.tensor_tensor(poly[:, g, :, :], poly[:, g, :, :], ex[:, g, :, :], ALU.mult).then_inc(s_poly, 1)

            def times_b(row, par, s):
                g = s // N
                pool.wait_ge(s_bsb, row * STEPS + s + 1)
                if s % N == 0:
                    pool.wait_ge(s_dx, row * 2 + g + 1)
                wait(pool, s_scan, row * 2 * STEPS + 2 * (s - RING) + 2)
                nc.gpsimd.tensor_tensor(bx[:, s % RING, :, :], dx[:, par, g, :, :],
                                        b_sb[:, s % RING, :].unsqueeze(1).broadcast_to([P, DT, T]),
                                        ALU.mult).then_inc(s_bx, 1)

            def residual(row):
                pool.wait_ge(s_yg, row * 2 + 2)
                pool.wait_ge(s_xr, row * 16 + 16)
                nc.gpsimd.tensor_tensor(og[:, :, :], og[:, :, :], xres[:, :, :], ALU.add).then_inc(s_out, 1)

            for g in range(2):
                polynomial(0, g)
            for g in range(2):
                step_x(0, 0, g)

            def body(row, par, last):
                for s in range(STEPS):
                    times_b(row, par, s)
                    if not last and s in (20, 22):
                        polynomial(row + 1, (s - 20) // 2)
                    if not last and s in (25, 28):
                        step_x(row + 1, 1 - par, (s - 25) // 3)
                    if s == 9 and not (isinstance(row, int) and row == 0):
                        residual(row - 1)
            rows(body)(pool)
            residual(NB - 1)

        @block.scalar
        def _(act):
            A = nc.scalar.activation
            exp_ln = "natural_log_exp_and_others"
            act.preload_act_table_set(exp_ln)
            def normalise_scale(row):
                act.wait_ge(s_mv, row * C + C)
                wait(act, s_shift, row)
                A(lnv[:, :], mv[:, :, 1], ACT.Ln, bias=eps[:, :]).then_inc(s_ln, 1)
                act.wait_ge(s_ln, row + 1)
                A(rs[:, :], lnv[:, :], ACT.Exp, scale=-0.5).then_inc(s_rs, 1)

            def normalise(row):
                act.wait_ge(s_shift, row + 1)
                wait(act, s_zz, row * 2)
                for c in range(C):
                    A(xn[:, c, :], xin[:, c, :], ACT.Identity, scale=rs[:, c:c + 1], bias=shift[:, c:c + 1]).then_inc(s_xn, 1)

            def copy_xnT(row, k):
                act.wait_ge(s_pf, row * UNITS + k + 1)
                if k == 0:
                    wait(act, s_skip, row * DT)
                    wait(act, s_dx, row * 2)
                A(xnT[:, k, :].rearrange("p (q c) -> p c q", c=C), fps[k][:, :].rearrange("p (c q) -> p c q", c=C),
                  ACT.Copy).then_inc(s_xnT, 1)

            def copy_delta_low(row):
                act.wait_ge(s_pf, row * UNITS + 3)
                A(dpr[:, :], fps[0][:, :], ACT.Copy).then_inc(s_dpr, 1)

            def high_part(row):
                wait(act, s_bc3, row * 96)
                A(high[:, :], fps[0][:, :], ACT.Copy).then_inc(s_hi, 1)

            def middle_part(row):
                act.wait_ge(s_rest, row + 1)
                A(mid[:, :], rest[:, :], ACT.Copy).then_inc(s_mid, 1)

            def absolute(row, par, q):
                g, k = q // DT, q % DT
                act.wait_ge(s_pf, row * UNITS + 4 + q)
                wait(act, s_poly, (row - 1) * 2 + g + 1)
                bank = fps[(3 + q) % 2]
                A(ex[:, g, k, :], bank[:, :], ACT.Abs, bias=dtb[:, g, k:k + 1]).then_inc(s_abs, 1)
                wait(act, s_dx, (row - 1) * 2)
                wait(act, s_decay, (row - 1) * 2 * STEPS)
                A(delta[:, par, g, k, :], bank[:, :], ACT.Relu, bias=dtb[:, g, k:k + 1]).then_inc(s_relu, 1)

            def exp_abs(row, g):
                act.wait_ge(s_abs, row * 4 + 2 * g + 2)
                A(ex[:, g, :, :], ex[:, g, :, :], ACT.Exp, scale=-1.0).then_inc(s_ex, 1)

            def log_one_plus(row, g):
                act.wait_ge(s_ex, row * 2 + g + 1)
                wait(act, s_delta, (row - 1) * 2 + g + 1)
                A(lg[:, g, :, :], ex[:, g, :, :], ACT.Ln, bias=1.0).then_inc(s_lg, 1)

            def square(row, g):
                act.wait_ge(s_ex, row * 2 + g + 1)
                wait(act, s_min, (row - 1) * 2 + g + 1)
                A(poly[:, g, :, :], ex[:, g, :, :], ACT.Square, scale=SQ_SCALE, bias=sq_shift[:, :]).then_inc(s_sq, 1)

            def hidden(row, j):
                act.wait_ge(s_pf, row * UNITS + 8 + j)
                if j == 0:
                    act.wait_ge(s_w, row * 64 + 64)
                A(hT[:, j, :], fps[(7 + j) % 2][:, :], ACT.Identity, bias=b1_sb[:, j:j + 1]).then_inc(s_hid, 1)

            def gelu(row):
                act.wait_ge(s_hid, row * FT + FT)
                A(hT[:, :, :], hT[:, :, :], ACT.Gelu).then_inc(s_gelu, 1)

            def silu(row):
                act.wait_ge(s_zz, row * 2 + 2)
                wait(act, s_yg, row * 2)
                A(gate[:, :, :], zz[:, :, :], ACT.Silu).then_inc(s_gate, 1)

            def front(row, par, s):
                if s == 2:
                    normalise_scale(row)
                if s == 4:
                    normalise(row)
                if s in (7, 8):
                    copy_xnT(row, s - 7)
                if s == 11:
                    copy_delta_low(row)
                    high_part(row)
                if s == 12:
                    middle_part(row)
                if s in (13, 14, 15, 16):
                    absolute(row, par, s - 13)
                if s in (15, 17):
                    exp_abs(row, (s - 15) // 2)
                if s in (16, 18):
                    square(row, (s - 16) // 2)
                if s in (17, 19):
                    log_one_plus(row, (s - 17) // 2)
                if s in (18, 20, 22, 24):
                    hidden(row, (s - 18) // 2)
                if s == 25:
                    gelu(row)

            act.wait_ge(s_const, 4)
            act.wait_ge(s_rv, 2)
            A(xl_ln[:, :], xl_mv[:, 1:2], ACT.Ln, bias=eps[0:NB, :]).then_inc(s_ra, 1)
            act.wait_ge(s_ra, 1)
            A(xl_rs[:, :], xl_ln[:, :], ACT.Exp, scale=-0.5).then_inc(s_ra, 1)
            act.wait_ge(s_rv, 3)
            A(xnl[:, :], xl[:, :], ACT.Identity, scale=xl_rs[:, :], bias=xl_shift[:, :]).then_inc(s_ra, 1)
            for s in range(5):
                front(0, 0, s)

            act.sem_inc(s_w2oc, 4)
            for a in range(2):
                act.sem_inc(s_w2st[a], 16)
            with act.Fori(1, NE // 2 + 1) as i:
                for a in range(2):
                    act.wait_ge(s_w2st[a], i * 16)
                    for h in range(2):
                        act.wait_ge(s_w2o, i * 4 + (2 * a + h - 3))
                        A(w2o_st[a][:, 2 * h:2 * h + 2, :], w2o_ps[a][h][:, :].rearrange("p (j d) -> p j d", j=2),
                          ACT.Copy).then_inc(s_w2oc, 1)

            act.wait_ge(s_rp, 2)
            A(hA[:, :], router_ps[:, 256:256 + NB], ACT.Gelu, bias=bp1_sb[:, :]).then_inc(s_ra, 1)
            act.preload_act_table_set(exp_ln)
            act.wait_ge(s_wload, 11 * 16)
            A(rate[:, :, :, :].rearrange("p a k n -> p (a k n)"), alog[:, :, :, :].rearrange("p a k n -> p (a k n)"),
              ACT.Exp).then_inc(s_aexp, 1)
            for s in (7, 8):
                front(0, 0, s)
            act.wait_ge(s_rv, 6)
            A(lexp[:, :], router_ps[0:NB, 384:384 + NE], ACT.Exp, bias=lneg[:, :], accum_out=lsum[:, :]).then_inc(s_ra, 1)

            def copy_b(row, s):
                act.wait_ge(s_bps, row * STEPS + s + 1)
                wait(act, s_bx, row * STEPS + s - RING + 1)
                A(b_sb[:, s % RING, :], bps[s % 2][:, :], ACT.Copy).then_inc(s_bsb, 1)

            def copy_y(row):
                act.wait_ge(s_red, row * STEPS + STEPS)
                wait(act, s_y, row * 2)
                for k in range(2):
                    A(ysb[:, k, :], yps[k][:, :], ACT.Copy).then_inc(s_yev, 1)

            for s in range(9, STEPS):
                front(0, 0, s)
            act.preload_act_table_set(exp_ln)
            def make_decay(row, par, s):
                g, n = s // N, s % N
                for k in range(DT):
                    if n == 0:
                        act.wait_ge(s_delta, row * 2 + g + 1)
                    wait(act, s_scan, row * 2 * STEPS + 2 * (s - RING) + k + 1)
                    A(decay[:, s % RING, k, :], delta[:, par, g, k, :], ACT.Exp, scale=rate[:, g, k, n:n + 1]).then_inc(s_decay, 1)

            act.wait_ge(s_rate, 1)
            for s in range(LEAD):
                make_decay(0, 0, s)
            for s in range(AHEAD - 1):
                copy_b(0, s)

            def body(row, par, last):
                for s in range(STEPS):
                    if s + LEAD < STEPS:
                        make_decay(row, par, s + LEAD)
                    elif not last:
                        make_decay(row + 1, 1 - par, s + LEAD - STEPS)
                    if s == 1 and not (isinstance(row, int) and row == 0):
                        copy_y(row - 1)
                    if s + AHEAD - 1 < STEPS:
                        copy_b(row, s + AHEAD - 1)
                    elif not last:
                        copy_b(row + 1, s + AHEAD - 1 - STEPS)
                    if not last:
                        front(row + 1, 1 - par, s)
                    if s == 25:
                        silu(row)
                        act.preload_act_table_set(exp_ln)
            rows(body)(act)
            copy_y(NB - 1)

        @block.vector
        def _(dve):
            V = nc.vector
            dve.wait_ge(s_ident, 1)
            V.tensor_tensor(sel3a[:, :], ident[0:96, 0:32], ident[0:96, 32:64], ALU.add).then_inc(s_sel, 1)
            dve.wait_ge(s_sel, 1)
            V.tensor_tensor(sel3[:, :], sel3a[:, :], ident[0:96, 64:96], ALU.add).then_inc(s_sel, 1)
            dve.wait_ge(s_sel, 2)
            V.tensor_copy(selector[:, :, :], sel3[:, :].unsqueeze(2).broadcast_to([96, 32, P])).then_inc(s_sel, 1)
            dve.wait_ge(s_rload, 5 * 16)
            V.bn_stats(xl_stats[:, :], xl[:, :]).then_inc(s_rv, 1)
            dve.wait_ge(s_rv, 1)
            V.bn_aggr(xl_mv[:, :], xl_stats[:, :]).then_inc(s_rv, 1)
            dve.wait_ge(s_ra, 2)
            V.scalar_tensor_tensor(xl_nwt[:, 0:1], xl_mv[:, 1:2], EPS, xl_rs[:, :], ALU.add, ALU.mult).then_inc(s_xnwt, 1)
            dve.wait_ge(s_xnwt, 1)
            V.scalar_tensor_tensor(xl_nwt[:, 1:2], xl_nwt[:, 0:1], -0.5, xl_rs[:, :], ALU.mult, ALU.mult).then_inc(s_xnwt, 1)
            dve.wait_ge(s_xnwt, 2)
            V.scalar_tensor_tensor(xl_rs[:, :], xl_nwt[:, 1:2], 1.5, xl_rs[:, :], ALU.add, ALU.mult).then_inc(s_xnwt, 1)
            dve.wait_ge(s_xnwt, 3)
            V.scalar_tensor_tensor(xl_shift[:, :], xl_mv[:, 0:1], -1.0, xl_rs[:, :], ALU.mult, ALU.mult).then_inc(s_rv, 1)
            def mean_variance(row):
                dve.wait_ge(s_x, row * 16 + 16)
                wait(dve, s_shift, row)
                for c in range(C):
                    V.bn_stats(stats[:, c, :], xin[:, c, :]).then_inc(s_bn, 1)
                wait_alone(dve, s_bn, row * C + C)
                for c in range(C):
                    V.bn_aggr(mv[:, c, :], stats[:, c, :]).then_inc(s_mv, 1)

            def shift_of(row):
                dve.wait_ge(s_rs, row + 1)
                wait(dve, s_xn, row * C)
                V.scalar_tensor_tensor(nwt[:, 0, :], mv[:, :, 1], EPS, rs[:, :], ALU.add, ALU.mult).then_inc(s_nwt, 1)
                dve.wait_ge(s_nwt, row * 3 + 1)
                V.scalar_tensor_tensor(nwt[:, 1, :], nwt[:, 0, :], -0.5, rs[:, :], ALU.mult, ALU.mult).then_inc(s_nwt, 1)
                dve.wait_ge(s_nwt, row * 3 + 2)
                V.scalar_tensor_tensor(rs[:, :], nwt[:, 1, :], 1.5, rs[:, :], ALU.add, ALU.mult).then_inc(s_nwt, 1)
                dve.wait_ge(s_nwt, row * 3 + 3)
                V.scalar_tensor_tensor(shift[:, :], mv[:, :, 0], -1.0, rs[:, :], ALU.mult, ALU.mult).then_inc(s_shift, 1)

            def rest_of(row):
                dve.wait_ge(s_hi, row + 1)
                V.tensor_tensor(rest[:, :], fps[0][:, :], high[:, :], ALU.subtract).then_inc(s_rest, 1)

            def low_part(row):
                dve.wait_ge(s_mid, row + 1)
                V.tensor_tensor(low[:, :], rest[:, :], mid[:, :], ALU.subtract).then_inc(s_lo, 1)

            def quadratic(row, g):
                dve.wait_ge(s_sq, row * 2 + g + 1)
                V.tensor_scalar(poly[:, g, :, :], poly[:, g, :, :], SQ_REST, None, ALU.add).then_inc(s_quad, 1)

            def log1p(row, g):
                dve.wait_ge(s_lg, row * 2 + g + 1)
                dve.wait_ge(s_poly, row * 2 + g + 1)
                V.scalar_tensor_tensor(lg[:, g, :, :], lg[:, g, :, :], LN_SLACK, poly[:, g, :, :],
                                       ALU.add, ALU.min).then_inc(s_min, 1)

            def step_size(row, par, g):
                dve.wait_ge(s_min, row * 2 + g + 1)
                dve.wait_ge(s_relu, row * 4 + 2 * g + 2)
                V.tensor_tensor(delta[:, par, g, :, :], lg[:, g, :, :], delta[:, par, g, :, :], ALU.add).then_inc(s_delta, 1)

            def gate_input(row, v):
                dve.wait_ge(s_pf, row * UNITS + 12 + v)
                if v == 0:
                    wait(dve, s_gate, row)
                V.scalar_tensor_tensor(zz[:, 2 * v:2 * v + 2, :], fps[1 - v][:, :].rearrange("p (c d) -> p c d", c=2), 0.3,
                                       xn[:, 2 * v:2 * v + 2, :], ALU.mult, ALU.add).then_inc(s_zz, 1)

            def front(row, par, s):
                if s == 0:
                    mean_variance(row)
                if s == 3:
                    shift_of(row)
                if s == 11:
                    rest_of(row)
                if s == 14:
                    low_part(row)
                if s in (17, 19):
                    quadratic(row, (s - 17) // 2)
                if s in (20, 22):
                    log1p(row, (s - 20) // 2)
                if s in (21, 24):
                    step_size(row, par, (s - 21) // 3)
                if s == 31:
                    gate_input(row, 0)

            def output(row, par, v):
                dve.wait_ge(s_y, row * 2 + v + 1)
                dve.wait_ge(s_gate, row + 1)
                wait(dve, s_store, row * 16)
                V.tensor_tensor(og[:, 2 * v:2 * v + 2, :], fps[1 - v][:, :].rearrange("p (c d) -> p c d", c=2), gate[:, 2 * v:2 * v + 2, :], ALU.mult).then_inc(s_yg, 1)

            def times_c(row, s):
                dve.wait_ge(s_scan, row * 2 * STEPS + 2 * s + 2)
                dve.wait_ge(s_cps, row * STEPS + s + 1)
                wait(dve, s_red, row * STEPS + s - RING + 1)
                V.tensor_tensor(hc[:, s % RING, :, :], hs[:, s % 2, :, :],
                                cps[s % 2][:, :].unsqueeze(1).broadcast_to([P, DT, T]), ALU.mult).then_inc(s_hc, 1)

            def scan(row, s, k):
                g = s // N
                u = slice(None) if g == 0 else slice(None, None, -1)
                dve.wait_ge(s_bx, row * STEPS + s + 1)
                dve.wait_ge(s_decay, row * 2 * STEPS + 2 * s + k + 1)
                wait(dve, s_hc, row * STEPS + s - 1)
                V.tensor_tensor_scan(hs[:, s % 2, k, u], decay[:, s % RING, k, u], bx[:, s % RING, k, u], 0.0,
                                     ALU.mult, ALU.add).then_inc(s_scan, 1)

            for s in range(4):
                front(0, 0, s)
            with dve.Fori(1, NE // 2 + 1) as i:
                for a in range(2):
                    for h in range(2):
                        dve.wait_ge(s_w2T, i * 4 + (2 * a + h - 3))
                        V.tensor_copy(ysb[:, h, :], w2T_ps[h][:, :]).then_inc(s_w2Tc, 1)
            dve.wait_ge(s_rp, 1)
            V.tensor_copy(xlT[:, :, :], router_ps[:, 0:DT * NB].rearrange("p (k b) -> p k b", k=DT)).then_inc(s_rv, 1)
            dve.wait_ge(s_wT, 1)
            V.tensor_copy(wx[:, :, :], weights_ps[:, 0:2 * P].rearrange("p (k m) -> p k m", k=DT)).then_inc(s_wev, 1)
            for g in range(2):
                V.tensor_copy(dtw[64 * g:64 * g + R, :, :],
                              weights_ps[64 * g:64 * g + R, 2 * P:4 * P].rearrange("r (k m) -> r k m", k=DT)).then_inc(s_wev, 1)
            V.tensor_tensor(dsum[:, :], dskip[:, 0, :], dskip[:, 1, :], ALU.add).then_inc(s_wev, 1)
            dve.wait_ge(s_wev, 4)
            for k in range(DT):
                V.tensor_scalar(diag_d[:, k, :], ident[:, :], dsum[:, k:k + 1], None, ALU.mult).then_inc(s_wev, 1)
            dve.wait_ge(s_rp, 3)
            V.max(lmax[:, :], router_ps[0:NB, 384:384 + NE]).then_inc(s_rv, 1)
            dve.wait_ge(s_rv, 5)
            V.tensor_scalar(lneg[:, :], lmax[:, 0:1], -1.0, None, ALU.mult).then_inc(s_rv, 1)
            dve.wait_ge(s_ra, 5)
            V.reciprocal(lrec[:, :], lsum[:, :]).then_inc(s_rv, 1)
            dve.wait_ge(s_rv, 7)
            V.tensor_scalar(probs[:, :], lexp[:, :], lrec[:, 0:1], None, ALU.mult).then_inc(s_rv, 1)
            dve.wait_ge(s_rv, 8)
            V.max(pmax[:, :], probs[:, :]).then_inc(s_rv, 1)
            dve.wait_ge(s_rv, 9)
            V.max_index(pidx[:, :], pmax[:, :], probs[:, :]).then_inc(s_rv, 1)
            dve.wait_ge(s_aexp, 1)
            V.tensor_scalar(rate[:, :, :, :].rearrange("p a k n -> p (a k n)"), rate[:, :, :, :].rearrange("p a k n -> p (a k n)"),
                            -1.0, None, ALU.mult).then_inc(s_rate, 1)
            dve.wait_ge(s_bias, 1)
            bias_sum = bias_ps[0:NE, 0:D]
            V.tensor_copy(bias_part[:, 0, :], bias_sum).then_inc(s_biasc, 1)
            dve.wait_ge(s_biasc, 1)
            V.tensor_tensor(bias_rest[:, :], bias_sum, bias_part[:, 0, :], ALU.subtract).then_inc(s_biasc, 1)
            dve.wait_ge(s_biasc, 2)
            V.tensor_copy(bias_part[:, 1, :], bias_rest[:, :]).then_inc(s_biasc, 1)
            dve.wait_ge(s_biasc, 3)
            V.tensor_tensor(bias_rest2[:, :], bias_rest[:, :], bias_part[:, 1, :], ALU.subtract).then_inc(s_biasc, 1)
            dve.wait_ge(s_biasc, 4)
            V.tensor_copy(bias_part[:, 2, :], bias_rest2[:, :]).then_inc(s_biasc, 1)

            for s in range(4, STEPS):
                front(0, 0, s)

            def body(row, par, last):
                for s in range(STEPS):
                    scan(row, s, 0)
                    if s:
                        times_c(row, s - 1)
                    scan(row, s, 1)
                    if s == 3:
                        gate_input(row, 1)
                    if s in (4, 6) and not (isinstance(row, int) and row == 0):
                        output(row - 1, 1 - par, (s - 4) // 2)
                    if not last:
                        front(row + 1, 1 - par, s)
                times_c(row, STEPS - 1)
            rows(body)(dve)
            for v in range(2):
                output(NB - 1, 1, v)

        @block.tensor
        def _(pe):
            M = nc.tensor.matmul
            pe.wait_ge(s_ident, 1)
            pe.wait_ge(s_wo, 16)
            with pe.Fori(1, NE // 2 + 1) as i:
                for a in range(2):
                    pe.wait_ge(s_w2[a], i * 16)
                    for h in range(2):
                        for j in range(2):
                            for k in range(DT):
                                ins = nc.tensor.transpose(w2T_ps[h][:, (j * DT + k) * P:(j * DT + k + 1) * P],
                                                          w2_in[a][:, 2 * h + j, k * P:(k + 1) * P], ident[:, :])
                        ins.then_inc(s_w2T, 1)
                    for h in range(2):
                        pe.wait_ge(s_w2Tc, i * 4 + (2 * a + h - 3))
                        pe.wait_ge(s_w2oc, i * 4 + (2 * a + h - 3))
                        for j in range(2):
                            for k in range(DT):
                                ins = M(w2o_ps[a][h][:, j * D:(j + 1) * D], w2T[:, 2 * h + j, k, :], wo_sb[:, k, :],
                                        start=(k == 0), stop=(k == DT - 1))
                        ins.then_inc(s_w2o, 1)

            def unit(row, u):
                if u < 2:
                    wait(pe, s_yg, (row - 1) * 2)
                elif u < 4:
                    pe.wait_ge(s_xnT, row * 2 + u - 1)
                elif u == 4:
                    pe.wait_ge(s_rest, row + 1)
                elif u < 9:
                    pe.wait_ge(s_relu, row * 4 + u - 4)
                else:
                    pe.wait_ge(s_hid, row * FT + u - 8)
                return fps[u % 2]

            def transpose_xn(row, k):
                bank = unit(row, k)
                pe.wait_ge(s_xn, row * C + C)
                for c in range(C):
                    ins = nc.tensor.transpose(bank[:, c * P:(c + 1) * P], xn[:, c, k * P:(k + 1) * P], ident[:, :])
                ins.then_inc(s_pf, 1)

            def project(row, k):
                if k == 0:
                    unit(row, 2)
                    pe.wait_ge(s_xnT, row * 2 + 2)
                ins = M(fps[0][:, :], wx[:, k, :], xnT[:, k, :], start=(k == 0), stop=(k == DT - 1))
                if k == DT - 1:
                    ins.then_inc(s_pf, 1)

            def expand_delta(row, q):
                g, k = q // DT, q % DT
                bank = unit(row, 3 + q)
                if q == 0:
                    pe.wait_ge(s_dpr, row + 1)
                M(bank[:, :], dtw[64 * g:64 * g + R, k, :], dpr[64 * g:64 * g + R, :], start=True, stop=True).then_inc(s_pf, 1)

            def ffn_in(row, j, k):
                if k == 0:
                    unit(row, 7 + j)
                    pe.wait_ge(s_w, row * 64 + 64)
                ins = M(fps[(7 + j) % 2][:, :], w1_sb[:, k, j * P:(j + 1) * P], xnT[:, k, :], start=(k == 0), stop=(k == DT - 1))
                if k == DT - 1:
                    ins.then_inc(s_pf, 1)

            def ffn_out(row, part):
                v, h, half = part // 4, part // 2 % 2, part % 2
                c, to = 2 * v + h, fps[1 - v][:, h * D:(h + 1) * D]
                if part % 4 == 0:
                    unit(row, 11 + v)
                    pe.wait_ge(s_gelu, row + 1)
                for j in range(half * 2, half * 2 + 2):
                    M(to, hT[:, j, :].rearrange("p (q c) -> p c q", c=C)[:, c, :], w2o_sb[:, j, :], start=(j == 0), stop=False)
                if half:
                    ins = M(to, ones3[:, :], bias3[:, :], start=False, stop=True)
                    if h:
                        ins.then_inc(s_pf, 1)

            def front(row, s):
                if s in (5, 6):
                    transpose_xn(row, s - 5)
                if s in (8, 9):
                    project(row, s - 8)
                if s in (11, 12, 13, 14):
                    expand_delta(row, s - 11)
                if 15 <= s < 23:
                    ffn_in(row, (s - 15) // 2, (s - 15) % 2)
                if s >= 26:
                    ffn_out(row, s - 26)

            def broadcast_b(row, par, s):
                wait(pe, s_bsb, row * STEPS + s - 1)
                if s == 0:
                    pe.wait_ge(s_bc3, row * 96 + 96)
                g, n = s // N, s % N
                M(bps[s % 2][:, :], selector[:, n, :], bc3[:, par, g, :], start=True, stop=True).then_inc(s_bps, 1)

            def broadcast_c(row, par, s):
                wait(pe, s_hc, row * STEPS + s - 1)
                g, n = s // N, s % N
                M(cps[s % 2][:, :], selector[:, N + n, :], bc3[:, par, g, :], start=True, stop=True).then_inc(s_cps, 1)

            def skip_term(row, k):
                M(yps[k][:, :], diag_d[:, k, :], xnT[:, k, :], start=False, stop=False).then_inc(s_skip, 1)

            def add_state(row, s):
                if s == 0:
                    wait(pe, s_yev, row * 2)
                pe.wait_ge(s_hc, row * STEPS + s + 1)
                for k in range(DT):
                    ins = M(yps[k][:, :], ident[:, :], hc[:, s % RING, k, :], start=(s == 0), stop=(s == STEPS - 1))
                ins.then_inc(s_red, 1)

            def tokens_of_y(row, v, last_front):
                pe.wait_ge(s_zz, last_front * 2 + 1 + v)
                pe.wait_ge(s_yev, row * 2 + 2)
                for h in range(2):
                    for k in range(DT):
                        to = fps[1 - v][:, h * D + k * P:h * D + (k + 1) * P]
                        ins = nc.tensor.transpose(to, ysb[:, k, :].rearrange("p (q c) -> p c q", c=C)[:, 2 * v + h, :], ident[:, :])
                ins.then_inc(s_y, 1)

            pe.wait_ge(s_ra, 3)
            pe.wait_ge(s_w2oc, 2 * NE + 4)
            for k in range(DT):
                ins = nc.tensor.transpose(router_ps[:, k * NB:(k + 1) * NB], xnl[:, k * P:(k + 1) * P], ident[0:NB, 0:NB])
            ins.then_inc(s_rp, 1)
            pe.wait_ge(s_wload, 11 * 16)
            for k in range(DT):
                nc.tensor.transpose(weights_ps[:, k * P:(k + 1) * P], xw_raw[:, k * P:(k + 1) * P], ident[:, :])
            for k in range(DT):
                ins = nc.tensor.transpose(weights_ps[:, (2 + k) * P:(3 + k) * P], dtw_raw[:, k, :], ident[:, :])
            ins.then_inc(s_wT, 1)
            pe.wait_ge(s_rload, 5 * 16)
            pe.wait_ge(s_rv, 4)
            for k in range(DT):
                ins = M(router_ps[:, 256:256 + NB], wp1_sb[:, k, :], xlT[:, k, :], start=(k == 0), stop=(k == DT - 1))
            ins.then_inc(s_rp, 1)
            for s in (5, 6):
                front(0, s)
            pe.wait_ge(s_b2T, 32)
            for k in range(DT):
                M(bias_ps[0:NE, 0:D], b2T[:, k, :], wo_sb[:, k, :], start=(k == 0), stop=False)
            M(bias_ps[0:NE, 0:D], ones_row[:, 0:NE], bo_row[:, :], start=False, stop=True).then_inc(s_bias, 1)
            pe.wait_ge(s_ra, 4)
            M(router_ps[0:NB, 384:384 + NE], hA[:, :], wp2_sb[:, :], start=True, stop=False)
            M(router_ps[0:NB, 384:384 + NE], ones_row[:, 0:NB], bp2_row[:, :], start=False, stop=True).then_inc(s_rp, 1)
            pe.wait_ge(s_sel, 3)
            pe.wait_ge(s_wev, 6)

            for s in range(8, STEPS):
                front(0, s)
            pe.wait_ge(s_biasc, 2)
            for s in range(AHEAD):
                broadcast_b(0, 0, s)
            broadcast_c(0, 0, 0)

            def body(row, par, last):
                for s in range(STEPS):
                    if s + 1 < STEPS:
                        broadcast_c(row, par, s + 1)
                    elif not last:
                        broadcast_c(row + 1, 1 - par, 0)
                    if s + AHEAD < STEPS:
                        broadcast_b(row, par, s + AHEAD)
                    elif not last:
                        broadcast_b(row + 1, 1 - par, s + AHEAD - STEPS)
                    if s < 2:
                        ffn_out(row, 6 + s)
                    if s in (2, 4) and not (isinstance(row, int) and row == 0):
                        tokens_of_y(row - 1, (s - 2) // 2, row)
                    if not last:
                        front(row + 1, s)
                    add_state(row, s)
                    if s < DT:
                        skip_term(row, s)
            rows(body)(pe)
            for v in range(2):
                tokens_of_y(NB - 1, v, NB - 1)


_INS = ["L0_attn_x", "L0_attn_x_proj_w", "L0_attn_dt_proj_w", "L0_attn_dt_proj_b", "L0_attn_A_log", "L0_attn_D",
        "L0_attn_x_proj_b_w", "L0_attn_dt_proj_b_w", "L0_attn_dt_proj_b_b", "L0_attn_A_b_log", "L0_attn_D_b",
        "L0_ffn_Wp1", "L0_ffn_bp1", "L0_ffn_Wp2", "L0_ffn_bp2", "L0_ffn_W1", "L0_ffn_b1", "L0_ffn_W2", "L0_ffn_b2",
        "L0_ffn_Wo", "L0_ffn_bo"]


def kernel(**inputs):
    import numpy as _np
    import concourse.bacc as _bacc
    from concourse.bass_utils import run_bass_kernel_spmd as _run

    nc = _bacc.Bacc("TRN2", target_bir_lowering=False, num_devices=1)
    arrays, args = {}, []
    for name in _INS:
        a = _np.ascontiguousarray(inputs[name])
        arrays[f"in_{name}_dram"] = a
        args.append(nc.dram_tensor(f"in_{name}_dram", a.shape, mybir.dt.from_np(a.dtype), kind="ExternalInput").ap())
    ne, f, d = inputs["L0_ffn_W2"].shape
    w2o = nc.dram_tensor("w2o_scratch", (ne, f, d), mybir.dt.float32, kind="Internal").ap()
    bias = nc.dram_tensor("bias_scratch", (ne, 3, d), mybir.dt.bfloat16, kind="Internal").ap()
    out = nc.dram_tensor("out_0_dram", inputs["L0_attn_x"].shape, mybir.dt.float32, kind="ExternalOutput").ap()
    mamba_moe_block(nc, *args, w2o, bias, out)
    r = _run(nc, [arrays], core_ids=[0])
    return r.results[0]["out_0_dram"]
```

```python
import concourse.bass as bass
from concourse import mybir
from contextlib import ExitStack


def mamba_moe_block(nc, x, xw_f, dtw_f, dtb_f, alog_f, d_f, xw_b, dtw_b, dtb_b, alog_b, d_b,
                    wp1, bp1, wp2, bp2, w1, b1, w2, b2, wo, bo,
                    w2o_dram, bias_dram, out):
    f32, bf16, u32 = mybir.dt.float32, mybir.dt.bfloat16, mybir.dt.uint32
    f32r = mybir.dt.float32r
    ALU, ACT = mybir.AluOpType, mybir.ActivationFunctionType

    NB, T, D = x.shape
    P = 128
    DT = D // P
    C = T // P
    N = alog_f.shape[1]
    R = dtw_f.shape[1]
    NE, _, F = w1.shape
    FT = F // P
    STEPS = 2 * N
    UNITS = 13
    RING = 4
    AHEAD = 5
    LEAD = 3
    UNIT_BANK = (0, 1, 0, 1, 0, 1, 0, 1, 0, 1, 0, 0, 1)
    MEAN, SCALE, SHIFT, NORM = 0, 0, 4, 5
    TRANS, XNT, PROJECT, HIGH, LOW = (6, 7), (7, 8), (8, 9), 10, 11
    EXPAND, ABS = (12, 13, 14, 15), (13, 14, 15, 16)
    EXP, SQUARE, QUAD, LN = (14, 30), (16, 34), (16, 34), (20, 33)
    POLY, LOG1P, STEPSIZE, DX = (22, 38), (21, 38), (23, 41), (29, 46)
    FFN_IN, HIDDEN, GELU = (16, 17, 18, 19, 20, 21, 22, 23), (19, 22, 25, 26), 28
    FFN_OUT, GATE = (29, 30, 31, 32, 33, 34, 35, 36), (35, 38)
    Y_COPY, Y_SKIP, Y_TOKENS, Y_OUT, Y_RESIDUAL = 0, 2, (4, 5), (7, 8), 11
    EPS = 1e-5
    LN_SLACK = 7e-8
    SQ_SCALE, SQ_SHIFT, SQ_REST = 3 ** -0.5, -(3 ** 0.5) / 4, 13 / 16

    ctx = ExitStack()
    with ctx:
        def sb(name, shape, dt=f32):
            return ctx.enter_context(nc.sbuf_tensor(name, shape, dt))

        def pb(name):
            return ctx.enter_context(nc.psum_tensor(name, [P, T], f32))

        def sem(name):
            return ctx.enter_context(nc.semaphore(name))

        ident = sb("ident", [P, P])
        selector = sb("selector", [P, 2 * N], f32r)
        ones_row = sb("ones_row", [1, P])
        eps = sb("eps", [P, 1])
        sq_shift = sb("sq_shift", [P, 1])
        sq_rest = sb("sq_rest", [P, 1])
        xw_raw = sb("xw_raw", [P, D])
        dtw_raw = sb("dtw_raw", [P, 2, DT, P])
        wx = sb("wx", [P, DT, P])
        dtw_high = sb("dtw_high", [P, 2, DT, P], f32r)
        dtw_low = sb("dtw_low", [P, 2, DT, P], f32r)
        dtb = sb("dtb", [P, 2, DT])
        alog = sb("alog", [P, 2, DT, N])
        rate = sb("rate", [P, 2, DT, N])
        dskip = sb("dskip", [P, 2, DT])
        dsum = sb("dsum", [P, DT])
        wo_sb = sb("wo_sb", [P, DT, D])
        bo_row = sb("bo_row", [1, D])
        b2T = sb("b2T", [P, DT, NE])
        bias_rest = sb("bias_rest", [NE, D])
        bias_rest2 = sb("bias_rest2", [NE, D])
        bias_part = sb("bias_part", [NE, 3, D], bf16)
        ones3 = sb("ones3", [3, P], bf16)
        xl = sb("xl", [NB, D])
        xl_stats = sb("xl_stats", [NB, 6])
        xl_mv = sb("xl_mv", [NB, 2])
        xl_ln = sb("xl_ln", [NB, 1])
        xl_rs = sb("xl_rs", [NB, 1])
        xl_nwt = sb("xl_nwt", [NB, 2])
        xl_shift = sb("xl_shift", [NB, 1])
        xnl = sb("xnl", [NB, D])
        xlT = sb("xlT", [P, DT, NB])
        wp1_sb = sb("wp1_sb", [P, DT, P])
        bp1_sb = sb("bp1_sb", [P, 1])
        wp2_sb = sb("wp2_sb", [P, NE])
        bp2_row = sb("bp2_row", [1, NE])
        hA = sb("hA", [P, NB])
        lmax = sb("lmax", [NB, 8])
        lneg = sb("lneg", [NB, 1])
        lexp = sb("lexp", [NB, NE])
        lsum = sb("lsum", [NB, 1])
        lrec = sb("lrec", [NB, 1])
        probs = sb("probs", [NB, NE])
        pmax = sb("pmax", [NB, 8])
        pidx = sb("pidx", [NB, 8], u32)
        expert_row = sb("expert_row", [1, NB], u32)
        xin = sb("xin", [P, C, D])
        stats = sb("stats", [P, C, 6])
        mv = sb("mv", [P, C, 2])
        lnv = sb("lnv", [P, C])
        rs = sb("rs", [P, C])
        nwt = sb("nwt", [P, 2, C])
        shift = sb("shift", [P, C])
        xn = sb("xn", [P, C, D])
        xnT = sb("xnT", [P, 2, DT, T])
        high = sb("high", [P, T], f32r)
        low = sb("low", [P, T], f32r)
        dbc = sb("dbc", [P, 2, 2, T], f32r)
        ex = sb("ex", [P, 2, DT, T])
        poly = sb("poly", [P, 2, DT, T])
        lg = sb("lg", [P, 2, DT, T])
        delta = sb("delta", [P, 2, 2, DT, T])
        dx = sb("dx", [P, 2, 2, DT, T])
        w1_sb = sb("w1_sb", [P, DT, F])
        w2o_sb = sb("w2o_sb", [P, FT, D])
        b1_sb = sb("b1_sb", [P, FT])
        bias3 = sb("bias3", [3, D], bf16)
        hT = sb("hT", [P, FT, T])
        zz = sb("zz", [P, C, D])
        gate = sb("gate", [P, C, D])
        b_sb = sb("b_sb", [P, RING, T])
        decay = sb("decay", [P, RING, DT, T])
        bx = sb("bx", [P, RING, DT, T])
        hs = sb("hs", [P, 2, DT, T])
        hc = sb("hc", [P, RING, DT, T])
        ysb = sb("ysb", [P, 2, T])
        xres = sb("xres", [P, C, D])
        og = sb("og", [P, C, D])
        w2_in = (w2o_sb, xres)
        w2T = ysb[:, :, :].rearrange("p a (j k f) -> p (a j) k f", k=DT, f=P)
        w2o_st = (og, gate)

        cps = [pb("c0"), pb("c1")]
        bps = [pb("b0"), pb("b1")]
        yps = [pb("y0"), pb("y1")]
        fps = [pb("front0"), pb("front1")]
        w2T_ps, w2o_ps = yps, (cps, bps)
        router_ps, wx_ps, dtw_ps, bias_ps = fps[1], bps[0], bps[1], fps[0]

        s_wload, s_rload = sem("weights_loaded"), sem("router_loaded")
        s_ident0, s_ident, s_const, s_sel = (sem(n) for n in ("ident0", "ident_ready", "const_ready", "sel_ready"))
        s_wT, s_wev, s_aexp, s_rate = (sem(n) for n in ("wT_ready", "wT_copied", "a_exp", "rate_ready"))
        s_rv, s_ra, s_rp = sem("router_dve"), sem("router_act"), sem("router_pe")
        s_sel_row = sem("expert_row_ready")
        s_x, s_xr, s_w = sem("x_loaded"), sem("xres_loaded"), sem("expert_loaded")
        s_bn, s_mv, s_ln, s_rs, s_shift = (sem(n) for n in ("bn_done", "mv_done", "ln_done", "rs_done", "shift_done"))
        s_xn, s_xnT = sem("xn_done"), sem("xnT_done")
        s_pf, s_hid = sem("front_unit_ready"), sem("hidden_copied")
        s_hi, s_lo = sem("high_done"), sem("low_done")
        s_abs, s_relu, s_ex, s_sq, s_lg = (sem(n) for n in ("abs_done", "relu_done", "ex_done", "square_done", "lg_done"))
        s_poly, s_min, s_delta, s_dx = (sem(n) for n in ("poly_done", "log1p_done", "delta_done", "dx_done"))
        s_gelu, s_zz, s_gate = (sem(n) for n in ("gelu_done", "zz_done", "gate_done"))
        s_dbc, s_quad = sem("dbc_moved"), sem("quadratic_done")
        s_nwt, s_xnwt = sem("newton_steps"), sem("router_newton_steps")
        s_wo, s_dsum = sem("wo_loaded"), sem("skip_weights_summed")
        s_w2, s_w2st = (sem("w2_loaded0"), sem("w2_loaded1")), (sem("w2o_stored0"), sem("w2o_stored1"))
        s_w2T, s_w2Tc, s_w2o, s_w2oc = (sem(n) for n in ("w2T_ready", "w2T_copied", "w2o_ready", "w2o_copied"))
        s_bias, s_biasc, s_biasst, s_b2T, s_dtz = (sem(n) for n in ("bias_ready", "bias_parts", "bias_stored", "b2T_loaded", "dtw_zeroed"))
        s_bps, s_bsb, s_bx = sem("b_psum"), sem("b_sbuf"), sem("bx_done")
        s_decay, s_scan, s_cps, s_hc, s_red = (sem(n) for n in ("decay_done", "scan_done", "c_psum", "hc_done", "sum_states_done"))
        s_skip = sem("skip_done")
        s_yev, s_y = sem("y_copied"), sem("y_tokens")
        s_passed = sem("wait_passed")
        s_yg, s_out, s_store = sem("yg_done"), sem("out_done"), sem("stored")

        def wait(eng, s, value):
            if not isinstance(value, int) or value > 0:
                eng.wait_ge(s, value)

        def wait_alone(eng, s, value):
            if not isinstance(value, int) or value > 0:
                eng.wait_ge(s, value)
                eng.sem_inc(s_passed, 1)

        def rows(body):
            def run(eng):
                for par in range(2):
                    body(par, par, False)
                if NB > 4:
                    with eng.Fori(1, NB // 2 - 1) as i:
                        for par in range(2):
                            body(i * 2 + par, par, False)
                for par in range(2):
                    body(NB - 2 + par, par, par == 1)
            return run

        x_rows = x.rearrange("b (p c) d -> b p (c d)", c=C)
        out_rows = out.rearrange("b (p c) d -> b p (c d)", c=C)
        w1_v = w1.rearrange("e (k p) f -> e p k f", p=P)
        w2_v = w2.rearrange("e (k p) d -> e p k d", p=P)
        b1_v = b1.rearrange("e (k p) -> e p k", p=P)
        w2o_v = w2o_dram.rearrange("e (k p) d -> e p k d", p=P)

        def one(view, row):
            return view[row] if isinstance(row, int) else view[bass.ds(row, 1)].squeeze(0)

        block = ctx.enter_context(nc.Block())

        @block.sync
        def _(sp):
            sp.dma_start(wo_sb[:, :, :], wo.rearrange("(k p) n -> p k n", p=P)).then_inc(s_wo, 16)
            for e in range(2):
                sp.dma_start(w2_in[e][:, :, :], w2_v[e]).then_inc(s_w2[e], 16)
            sp.dma_start(xin[:, :, :], x_rows[0].rearrange("p (c d) -> p c d", c=C)).then_inc(s_x, 16)
            sp.dma_start(xl[:, :], x[:, T - 1, :]).then_inc(s_rload, 16)
            sp.dma_start(wp1_sb[:, :, :], wp1.rearrange("(k p) n -> p k n", p=P)).then_inc(s_rload, 16)
            sp.dma_start(bp1_sb[:, :], bp1.rearrange("(p a) -> p a", a=1)).then_inc(s_rload, 16)
            sp.dma_start(wp2_sb[:, :], wp2).then_inc(s_rload, 16)
            sp.dma_start(bp2_row[:, :], bp2.rearrange("(a n) -> a n", a=1)).then_inc(s_rload, 16)
            for g, w in enumerate((xw_f, xw_b)):
                sp.dma_start(xw_raw[64 * g:64 * g + 64, :], w).then_inc(s_wload, 16)
            sp.wait_ge(s_dtz, 1)
            for g, w in enumerate((dtw_f, dtw_b)):
                for a in range(2):
                    sp.dma_start(dtw_raw[:, g, :, 64 * a:64 * a + R], w.rearrange("(k p) r -> p k r", p=P)).then_inc(s_wload, 16)
            for g, (bias, al, dd) in enumerate(((dtb_f, alog_f, d_f), (dtb_b, alog_b, d_b))):
                sp.dma_start(dtb[:, g, :], bias.rearrange("(k p) -> p k", p=P), allow_slow_non_contiguous=True).then_inc(s_wload, 16)
                sp.dma_start(alog[:, g, :, :], al.rearrange("(k p) n -> p k n", p=P)).then_inc(s_wload, 16)
                sp.dma_start(dskip[:, g, :], dd.rearrange("(k p) -> p k", p=P), allow_slow_non_contiguous=True).then_inc(s_wload, 16)
            sp.dma_start(bo_row[:, :], bo.rearrange("(a n) -> a n", a=1)).then_inc(s_wload, 16)

            for k in range(DT):
                sp.dma_start(b2T[:, k, :], b2[:, k * P:(k + 1) * P].rearrange("e p -> p e"),
                             allow_slow_non_contiguous=True).then_inc(s_b2T, 16)

            for pair in range(NE // 2):
                for a in range(2):
                    e = 2 * pair + a
                    if e + 2 < NE:
                        sp.wait_ge(s_w2T, 2 * e + 2)
                        sp.dma_start(w2_in[a][:, :, :], w2_v[e + 2]).then_inc(s_w2[a], 16)
                    sp.wait_ge(s_w2oc, 2 * e + 2)
                    sp.dma_start(w2o_v[e], w2o_st[a][:, :, :]).then_inc(s_w2st[a], 16)
            sp.wait_ge(s_biasc, 5)
            sp.dma_start(bias_dram, bias_part[:, :, :]).then_inc(s_biasst, 16)

            sp.wait_ge(s_rv, 10)
            sp.dma_start(expert_row[:, :], pidx[:, 0:1], allow_slow_non_contiguous=True).then_inc(s_sel_row, 16)
            sp.wait_ge(s_biasst, 16)
            for a in range(2):
                sp.wait_ge(s_w2st[a], 16 * (NE // 2))
            sp.wait_ge(s_sel_row, 16)

            def load_expert(row):
                wait_alone(sp, s_pf, row * UNITS)
                wait_alone(sp, s_gelu, row)
                sel = sp.value_load(expert_row[0:1, row:row + 1] if isinstance(row, int) else expert_row[0:1, bass.ds(row, 1)],
                                    min_val=0, max_val=NE - 1)
                sp.dma_start(w1_sb[:, :, :], one(w1_v, sel)).then_inc(s_w, 16)
                sp.dma_start(w2o_sb[:, :, :], one(w2o_v, sel)).then_inc(s_w, 16)
                sp.dma_start(b1_sb[:, :], one(b1_v, sel), allow_slow_non_contiguous=True).then_inc(s_w, 16)
                sp.dma_start(bias3[:, :], one(bias_dram, sel)).then_inc(s_w, 16)

            def load_x(row):
                wait_alone(sp, s_xn, row * C)
                sp.dma_start(xin[:, :, :].rearrange("p c d -> p (c d)"), one(x_rows, row)).then_inc(s_x, 16)

            def store(row):
                wait_alone(sp, s_out, row + 1)
                sp.dma_start(one(out_rows, row), og[:, :, :].rearrange("p c d -> p (c d)")).then_inc(s_store, 16)

            def load_residual(row):
                wait_alone(sp, s_out, row)
                sp.dma_start(xres[:, :, :].rearrange("p c d -> p (c d)"), one(x_rows, row)).then_inc(s_xr, 16)

            def move_bc(row, par):
                wait_alone(sp, s_bps, (row - 1) * STEPS)
                wait_alone(sp, s_cps, (row - 1) * STEPS)
                wait_alone(sp, s_lo, row + 1)
                for g in range(2):
                    for a, part in enumerate((high, low)):
                        sp.dma_start(dbc[64 * a:64 * a + 64, par, g, :].bitcast(f32),
                                     part[64 * g:64 * g + 64, :].bitcast(f32)).then_inc(s_dbc, 16)

            load_expert(0)
            move_bc(0, 0)

            def body(row, par, last):
                if not last:
                    load_x(row + 1)
                    load_expert(row + 1)
                if isinstance(row, int) and row == 0:
                    load_residual(row)
                else:
                    store(row - 1)
                    load_residual(row)
                if not last:
                    move_bc(row + 1, 1 - par)
            rows(body)(sp)
            store(NB - 1)
            sp.wait_ge(s_store, 16 * NB)

        @block.gpsimd
        def _(pool):
            nc.gpsimd.memset(ident[:, :], 0.0).then_inc(s_ident0, 1)
            nc.gpsimd.memset(ones_row[:, :], 1.0).then_inc(s_const, 1)
            nc.gpsimd.memset(eps[:, :], EPS).then_inc(s_const, 1)
            nc.gpsimd.memset(sq_shift[:, :], SQ_SHIFT).then_inc(s_const, 1)
            nc.gpsimd.memset(sq_rest[:, :], SQ_REST).then_inc(s_const, 1)
            nc.gpsimd.memset(ones3[:, :], 1.0).then_inc(s_const, 1)
            nc.gpsimd.memset(dtw_raw[:, :, :, :], 0.0).then_inc(s_dtz, 1)
            pool.wait_ge(s_ident0, 1)
            nc.gpsimd.affine_select(out=ident[:, :], in_=ident[:, :], compare_op=ALU.not_equal, fill=1.0, base=0,
                                    pattern=[[-1, P]], channel_multiplier=1).then_inc(s_ident, 1)

            def step_x(row, par, g):
                pool.wait_ge(s_delta, row * 2 + g + 1)
                pool.wait_ge(s_xnT, row * 2 + 2)
                wait(pool, s_bx, (row - 1) * STEPS)
                nc.gpsimd.tensor_tensor(dx[:, par, g, :, :], delta[:, par, g, :, :], xnT[:, par, :, :], ALU.mult).then_inc(s_dx, 1)

            def polynomial(row, g):
                pool.wait_ge(s_quad, row * 2 + g + 1)
                nc.gpsimd.tensor_tensor(poly[:, g, :, :], poly[:, g, :, :], ex[:, g, :, :], ALU.mult).then_inc(s_poly, 1)

            def times_b(row, par, s):
                g = s // N
                pool.wait_ge(s_bsb, row * STEPS + s + 1)
                if s % N == 0:
                    pool.wait_ge(s_dx, row * 2 + g + 1)
                wait(pool, s_scan, row * 2 * STEPS + 2 * (s - RING) + 2)
                nc.gpsimd.tensor_tensor(bx[:, s % RING, :, :], dx[:, par, g, :, :],
                                        b_sb[:, s % RING, :].unsqueeze(1).broadcast_to([P, DT, T]),
                                        ALU.mult).then_inc(s_bx, 1)

            def residual(row):
                pool.wait_ge(s_yg, row * 2 + 2)
                pool.wait_ge(s_xr, row * 16 + 16)
                nc.gpsimd.tensor_tensor(og[:, :, :], og[:, :, :], xres[:, :, :], ALU.add).then_inc(s_out, 1)

            def front(row, par, s):
                if s in POLY:
                    polynomial(row, POLY.index(s))
                if s in DX:
                    step_x(row, par, DX.index(s))

            for s in range(STEPS):
                front(0, 0, s)

            def body(row, par, last):
                for s in range(STEPS):
                    times_b(row, par, s)
                    front(row, par, s + STEPS)
                    if not last:
                        front(row + 1, 1 - par, s)
                    if s == Y_RESIDUAL and not (isinstance(row, int) and row == 0):
                        residual(row - 1)
            rows(body)(pool)
            residual(NB - 1)

        @block.scalar
        def _(act):
            A = nc.scalar.activation
            exp_ln = "natural_log_exp_and_others"
            act.preload_act_table_set(exp_ln)
            def normalise_scale(row):
                act.wait_ge(s_mv, row * C + C)
                wait(act, s_shift, row)
                A(lnv[:, :], mv[:, :, 1], ACT.Ln, bias=eps[:, :]).then_inc(s_ln, 1)
                act.wait_ge(s_ln, row + 1)
                A(rs[:, :], lnv[:, :], ACT.Exp, scale=-0.5).then_inc(s_rs, 1)

            def normalise(row):
                act.wait_ge(s_shift, row + 1)
                wait(act, s_zz, row * 2)
                for c in range(C):
                    A(xn[:, c, :], xin[:, c, :], ACT.Identity, scale=rs[:, c:c + 1], bias=shift[:, c:c + 1]).then_inc(s_xn, 1)

            def copy_xnT(row, par, k):
                act.wait_ge(s_pf, row * UNITS + k + 1)
                if k == 0:
                    wait(act, s_skip, (row - 1) * DT)
                    wait(act, s_dx, (row - 1) * 2)
                A(xnT[:, par, k, :].rearrange("p (q c) -> p c q", c=C), fps[UNIT_BANK[k]][:, :].rearrange("p (c q) -> p c q", c=C),
                  ACT.Copy).then_inc(s_xnT, 1)

            def high_part(row):
                act.wait_ge(s_pf, row * UNITS + 3)
                wait(act, s_dbc, row * 64)
                A(high[:, :], fps[UNIT_BANK[2]][:, :], ACT.Copy).then_inc(s_hi, 1)

            def absolute(row, par, q):
                g, k = q // DT, q % DT
                act.wait_ge(s_pf, row * UNITS + 4 + q)
                wait(act, s_poly, (row - 1) * 2 + g + 1)
                bank = fps[UNIT_BANK[3 + q]]
                A(ex[:, g, k, :], bank[:, :], ACT.Abs, bias=dtb[:, g, k:k + 1]).then_inc(s_abs, 1)
                wait(act, s_dx, (row - 1) * 2)
                wait(act, s_decay, (row - 1) * 2 * STEPS)
                A(delta[:, par, g, k, :], bank[:, :], ACT.Relu, bias=dtb[:, g, k:k + 1]).then_inc(s_relu, 1)

            def exp_abs(row, g):
                act.wait_ge(s_abs, row * 4 + 2 * g + 2)
                A(ex[:, g, :, :], ex[:, g, :, :], ACT.Exp, scale=-1.0).then_inc(s_ex, 1)

            def log_one_plus(row, g):
                act.wait_ge(s_ex, row * 2 + g + 1)
                wait(act, s_delta, (row - 1) * 2 + g + 1)
                A(lg[:, g, :, :], ex[:, g, :, :], ACT.Ln, bias=1.0).then_inc(s_lg, 1)

            def square(row, g):
                act.wait_ge(s_ex, row * 2 + g + 1)
                wait(act, s_min, (row - 1) * 2 + g + 1)
                A(poly[:, g, :, :], ex[:, g, :, :], ACT.Square, scale=SQ_SCALE, bias=sq_shift[:, :]).then_inc(s_sq, 1)

            def quadratic(row, g):
                act.wait_ge(s_sq, row * 2 + g + 1)
                A(poly[:, g, :, :], poly[:, g, :, :], ACT.Identity, bias=sq_rest[:, :]).then_inc(s_quad, 1)

            def hidden(row, j):
                act.wait_ge(s_pf, row * UNITS + 8 + j)
                if j == 0:
                    act.wait_ge(s_w, row * 64 + 64)
                A(hT[:, j, :], fps[UNIT_BANK[7 + j]][:, :], ACT.Identity, bias=b1_sb[:, j:j + 1]).then_inc(s_hid, 1)

            def gelu(row):
                act.wait_ge(s_hid, row * FT + FT)
                A(hT[:, :, :], hT[:, :, :], ACT.Gelu).then_inc(s_gelu, 1)

            def silu(row):
                act.wait_ge(s_zz, row * 2 + 2)
                wait(act, s_yg, row * 2)
                A(gate[:, :, :], zz[:, :, :], ACT.Silu).then_inc(s_gate, 1)

            def front(row, par, s):
                if s == SCALE:
                    normalise_scale(row)
                if s == NORM:
                    normalise(row)
                if s in XNT:
                    copy_xnT(row, par, XNT.index(s))
                if s == HIGH:
                    high_part(row)
                if s in ABS:
                    absolute(row, par, ABS.index(s))
                if s in EXP:
                    exp_abs(row, EXP.index(s))
                if s in SQUARE:
                    square(row, SQUARE.index(s))
                if s in QUAD:
                    quadratic(row, QUAD.index(s))
                if s in LN:
                    log_one_plus(row, LN.index(s))
                if s in HIDDEN:
                    hidden(row, HIDDEN.index(s))
                if s == GELU:
                    gelu(row)

            def copy_w2o(pair):
                for a in range(2):
                    wait(act, s_w2st[a], pair * 16)
                    for h in range(2):
                        act.wait_ge(s_w2o, pair * 4 + 2 * a + h + 1)
                        A(w2o_st[a][:, 2 * h:2 * h + 2, :], w2o_ps[a][h][:, :].rearrange("p (j d) -> p j d", j=2),
                          ACT.Copy).then_inc(s_w2oc, 1)

            act.wait_ge(s_const, 5)
            for pair in range(NE // 2):
                copy_w2o(pair)
                if pair == 0:
                    act.wait_ge(s_rv, 2)
                    A(xl_ln[:, :], xl_mv[:, 1:2], ACT.Ln, bias=eps[0:NB, :]).then_inc(s_ra, 1)
                    act.wait_ge(s_ra, 1)
                    A(xl_rs[:, :], xl_ln[:, :], ACT.Exp, scale=-0.5).then_inc(s_ra, 1)
                    for s in range(SCALE + 1):
                        front(0, 0, s)
                if pair == 1:
                    act.wait_ge(s_rv, 3)
                    A(xnl[:, :], xl[:, :], ACT.Identity, scale=xl_rs[:, :], bias=xl_shift[:, :]).then_inc(s_ra, 1)
                    for s in range(SCALE + 1, NORM + 1):
                        front(0, 0, s)
                if pair == 2:
                    act.wait_ge(s_wload, 13 * 16)
                    A(rate[:, :, :, :].rearrange("p a k n -> p (a k n)"), alog[:, :, :, :].rearrange("p a k n -> p (a k n)"),
                      ACT.Exp).then_inc(s_aexp, 1)

            act.wait_ge(s_rp, 2)
            A(hA[:, :], router_ps[:, 256:256 + NB], ACT.Gelu, bias=bp1_sb[:, :]).then_inc(s_ra, 1)
            act.preload_act_table_set(exp_ln)
            act.wait_ge(s_rv, 6)
            A(lexp[:, :], router_ps[0:NB, 384:384 + NE], ACT.Exp, bias=lneg[:, :], accum_out=lsum[:, :]).then_inc(s_ra, 1)
            for s in range(NORM + 1, XNT[1] + 1):
                front(0, 0, s)

            def copy_b(row, s):
                act.wait_ge(s_bps, row * STEPS + s + 1)
                wait(act, s_bx, row * STEPS + s - RING + 1)
                A(b_sb[:, s % RING, :], bps[s % 2][:, :], ACT.Copy).then_inc(s_bsb, 1)

            def copy_y(row):
                act.wait_ge(s_red, row * STEPS + STEPS)
                wait(act, s_y, row * 2)
                for k in range(2):
                    A(ysb[:, k, :], yps[k][:, :], ACT.Copy).then_inc(s_yev, 1)

            for s in range(XNT[1] + 1, STEPS):
                front(0, 0, s)
            act.preload_act_table_set(exp_ln)
            def make_decay(row, par, s):
                g, n = s // N, s % N
                for k in range(DT):
                    if n == 0:
                        act.wait_ge(s_delta, row * 2 + g + 1)
                    wait(act, s_scan, row * 2 * STEPS + 2 * (s - RING) + k + 1)
                    A(decay[:, s % RING, k, :], delta[:, par, g, k, :], ACT.Exp, scale=rate[:, g, k, n:n + 1]).then_inc(s_decay, 1)

            act.wait_ge(s_rate, 1)
            for s in range(LEAD):
                make_decay(0, 0, s)
            for s in range(AHEAD - 1):
                copy_b(0, s)

            def body(row, par, last):
                for s in range(STEPS):
                    if s + LEAD < STEPS:
                        make_decay(row, par, s + LEAD)
                    elif not last:
                        make_decay(row + 1, 1 - par, s + LEAD - STEPS)
                    if s == Y_COPY and not (isinstance(row, int) and row == 0):
                        copy_y(row - 1)
                    if s + AHEAD - 1 < STEPS:
                        copy_b(row, s + AHEAD - 1)
                    elif not last:
                        copy_b(row + 1, s + AHEAD - 1 - STEPS)
                    front(row, par, s + STEPS)
                    if not last:
                        front(row + 1, 1 - par, s)
                    if s == GELU:
                        silu(row)
                        act.preload_act_table_set(exp_ln)
            rows(body)(act)
            copy_y(NB - 1)

        @block.vector
        def _(dve):
            V = nc.vector
            dve.wait_ge(s_ident, 1)
            V.tensor_tensor(selector[:, :], ident[:, R:64], ident[:, 64 + R:P], ALU.add).then_inc(s_sel, 1)
            def mean_variance(row):
                dve.wait_ge(s_x, row * 16 + 16)
                wait(dve, s_shift, row)
                for c in range(C):
                    V.bn_stats(stats[:, c, :], xin[:, c, :]).then_inc(s_bn, 1)
                wait_alone(dve, s_bn, row * C + C)
                for c in range(C):
                    V.bn_aggr(mv[:, c, :], stats[:, c, :]).then_inc(s_mv, 1)

            def shift_of(row):
                dve.wait_ge(s_rs, row + 1)
                wait(dve, s_xn, row * C)
                V.scalar_tensor_tensor(nwt[:, 0, :], mv[:, :, 1], EPS, rs[:, :], ALU.add, ALU.mult).then_inc(s_nwt, 1)
                dve.wait_ge(s_nwt, row * 3 + 1)
                V.scalar_tensor_tensor(nwt[:, 1, :], nwt[:, 0, :], -0.5, rs[:, :], ALU.mult, ALU.mult).then_inc(s_nwt, 1)
                dve.wait_ge(s_nwt, row * 3 + 2)
                V.scalar_tensor_tensor(rs[:, :], nwt[:, 1, :], 1.5, rs[:, :], ALU.add, ALU.mult).then_inc(s_nwt, 1)
                dve.wait_ge(s_nwt, row * 3 + 3)
                V.scalar_tensor_tensor(shift[:, :], mv[:, :, 0], -1.0, rs[:, :], ALU.mult, ALU.mult).then_inc(s_shift, 1)

            def low_part(row):
                dve.wait_ge(s_hi, row + 1)
                V.tensor_tensor(low[:, :], fps[UNIT_BANK[2]][:, :], high[:, :], ALU.subtract).then_inc(s_lo, 1)

            def log1p(row, g):
                dve.wait_ge(s_lg, row * 2 + g + 1)
                dve.wait_ge(s_poly, row * 2 + g + 1)
                V.scalar_tensor_tensor(lg[:, g, :, :], lg[:, g, :, :], LN_SLACK, poly[:, g, :, :],
                                       ALU.add, ALU.min).then_inc(s_min, 1)

            def step_size(row, par, g):
                dve.wait_ge(s_min, row * 2 + g + 1)
                dve.wait_ge(s_relu, row * 4 + 2 * g + 2)
                V.tensor_tensor(delta[:, par, g, :, :], lg[:, g, :, :], delta[:, par, g, :, :], ALU.add).then_inc(s_delta, 1)

            def gate_input(row, v):
                dve.wait_ge(s_pf, row * UNITS + 12 + v)
                if v == 0:
                    wait(dve, s_gate, row)
                V.scalar_tensor_tensor(zz[:, 2 * v:2 * v + 2, :], fps[UNIT_BANK[11 + v]][:, :].rearrange("p (c d) -> p c d", c=2), 0.3,
                                       xn[:, 2 * v:2 * v + 2, :], ALU.mult, ALU.add).then_inc(s_zz, 1)

            def front(row, par, s):
                if s == MEAN:
                    mean_variance(row)
                if s == SHIFT:
                    shift_of(row)
                if s == LOW:
                    low_part(row)
                if s in LOG1P:
                    log1p(row, LOG1P.index(s))
                if s in STEPSIZE:
                    step_size(row, par, STEPSIZE.index(s))
                if s in GATE:
                    gate_input(row, GATE.index(s))

            def skip_term(row, par):
                dve.wait_ge(s_dsum, 1)
                for k in range(DT):
                    dve.wait_ge(s_yev, row * DT + k + 1)
                    V.scalar_tensor_tensor(ysb[:, k, :], xnT[:, par, k, :], dsum[:, k:k + 1], ysb[:, k, :],
                                           ALU.mult, ALU.add).then_inc(s_skip, 1)

            def output(row, par, v):
                dve.wait_ge(s_y, row * 2 + v + 1)
                dve.wait_ge(s_gate, row + 1)
                wait(dve, s_store, row * 16)
                V.tensor_tensor(og[:, 2 * v:2 * v + 2, :], fps[v][:, :].rearrange("p (c d) -> p c d", c=2), gate[:, 2 * v:2 * v + 2, :], ALU.mult).then_inc(s_yg, 1)

            def times_c(row, s):
                dve.wait_ge(s_scan, row * 2 * STEPS + 2 * s + 2)
                dve.wait_ge(s_cps, row * STEPS + s + 1)
                wait(dve, s_red, row * STEPS + s - RING + 1)
                V.tensor_tensor(hc[:, s % RING, :, :], hs[:, s % 2, :, :],
                                cps[s % 2][:, :].unsqueeze(1).broadcast_to([P, DT, T]), ALU.mult).then_inc(s_hc, 1)

            def scan(row, s, k):
                g = s // N
                u = slice(None) if g == 0 else slice(None, None, -1)
                dve.wait_ge(s_bx, row * STEPS + s + 1)
                dve.wait_ge(s_decay, row * 2 * STEPS + 2 * s + k + 1)
                wait(dve, s_hc, row * STEPS + s - 1)
                V.tensor_tensor_scan(hs[:, s % 2, k, u], decay[:, s % RING, k, u], bx[:, s % RING, k, u], 0.0,
                                     ALU.mult, ALU.add).then_inc(s_scan, 1)

            def copy_w2T(pair):
                for a in range(2):
                    for h in range(2):
                        dve.wait_ge(s_w2T, pair * 4 + 2 * a + h + 1)
                        V.tensor_copy(ysb[:, h, :], w2T_ps[h][:, :]).then_inc(s_w2Tc, 1)

            for pair in range(NE // 2):
                copy_w2T(pair)
                if pair == 0:
                    dve.wait_ge(s_rload, 5 * 16)
                    V.bn_stats(xl_stats[:, :], xl[:, :]).then_inc(s_rv, 1)
                    dve.wait_ge(s_rv, 1)
                    V.bn_aggr(xl_mv[:, :], xl_stats[:, :]).then_inc(s_rv, 1)
                    for s in range(MEAN + 1):
                        front(0, 0, s)
                if pair == 1:
                    dve.wait_ge(s_ra, 2)
                    V.scalar_tensor_tensor(xl_nwt[:, 0:1], xl_mv[:, 1:2], EPS, xl_rs[:, :], ALU.add, ALU.mult).then_inc(s_xnwt, 1)
                    dve.wait_ge(s_xnwt, 1)
                    V.scalar_tensor_tensor(xl_nwt[:, 1:2], xl_nwt[:, 0:1], -0.5, xl_rs[:, :], ALU.mult, ALU.mult).then_inc(s_xnwt, 1)
                    dve.wait_ge(s_xnwt, 2)
                    V.scalar_tensor_tensor(xl_rs[:, :], xl_nwt[:, 1:2], 1.5, xl_rs[:, :], ALU.add, ALU.mult).then_inc(s_xnwt, 1)
                    dve.wait_ge(s_xnwt, 3)
                    V.scalar_tensor_tensor(xl_shift[:, :], xl_mv[:, 0:1], -1.0, xl_rs[:, :], ALU.mult, ALU.mult).then_inc(s_rv, 1)
                    for s in range(MEAN + 1, SHIFT + 1):
                        front(0, 0, s)
                    dve.wait_ge(s_bias, 1)
                    bias_sum = bias_ps[0:NE, 0:D]
                    V.tensor_copy(bias_part[:, 0, :], bias_sum).then_inc(s_biasc, 1)
                    dve.wait_ge(s_biasc, 1)
                    V.tensor_tensor(bias_rest[:, :], bias_sum, bias_part[:, 0, :], ALU.subtract).then_inc(s_biasc, 1)
                    dve.wait_ge(s_biasc, 2)
                    V.tensor_copy(bias_part[:, 1, :], bias_rest[:, :]).then_inc(s_biasc, 1)
                    dve.wait_ge(s_biasc, 3)
                    V.tensor_tensor(bias_rest2[:, :], bias_rest[:, :], bias_part[:, 1, :], ALU.subtract).then_inc(s_biasc, 1)
                    dve.wait_ge(s_biasc, 4)
                    V.tensor_copy(bias_part[:, 2, :], bias_rest2[:, :]).then_inc(s_biasc, 1)
                if pair == 2:
                    dve.wait_ge(s_rp, 1)
                    V.tensor_copy(xlT[:, :, :], router_ps[:, 0:DT * NB].rearrange("p (k b) -> p k b", k=DT)).then_inc(s_rv, 1)
                    dve.wait_ge(s_aexp, 1)
                    V.tensor_scalar(rate[:, :, :, :].rearrange("p a k n -> p (a k n)"), rate[:, :, :, :].rearrange("p a k n -> p (a k n)"),
                                    -1.0, None, ALU.mult).then_inc(s_rate, 1)
                    V.tensor_tensor(dsum[:, :], dskip[:, 0, :], dskip[:, 1, :], ALU.add).then_inc(s_dsum, 1)
            dve.wait_ge(s_rp, 3)
            V.max(lmax[:, :], router_ps[0:NB, 384:384 + NE]).then_inc(s_rv, 1)
            dve.wait_ge(s_rv, 5)
            V.tensor_scalar(lneg[:, :], lmax[:, 0:1], -1.0, None, ALU.mult).then_inc(s_rv, 1)
            dve.wait_ge(s_ra, 5)
            V.reciprocal(lrec[:, :], lsum[:, :]).then_inc(s_rv, 1)
            dve.wait_ge(s_rv, 7)
            V.tensor_scalar(probs[:, :], lexp[:, :], lrec[:, 0:1], None, ALU.mult).then_inc(s_rv, 1)
            dve.wait_ge(s_rv, 8)
            V.max(pmax[:, :], probs[:, :]).then_inc(s_rv, 1)
            dve.wait_ge(s_rv, 9)
            V.max_index(pidx[:, :], pmax[:, :], probs[:, :]).then_inc(s_rv, 1)
            dve.wait_ge(s_wT, 1)
            V.tensor_copy(wx[:, :, :], wx_ps[:, 0:2 * P].rearrange("p (k m) -> p k m", k=DT)).then_inc(s_wev, 1)
            dtw_sum = dtw_ps[:, :].rearrange("r (g k m) -> r g k m", g=2, k=DT)
            V.tensor_copy(dtw_high[:, :, :, :], dtw_sum).then_inc(s_wev, 1)
            dve.wait_ge(s_wev, 2)
            V.tensor_tensor(dtw_low[:, :, :, :], dtw_sum, dtw_high[:, :, :, :], ALU.subtract).then_inc(s_wev, 1)
            for s in range(SHIFT + 1, STEPS):
                front(0, 0, s)

            def body(row, par, last):
                for s in range(STEPS):
                    scan(row, s, 0)
                    if s:
                        times_c(row, s - 1)
                    scan(row, s, 1)
                    front(row, par, s + STEPS)
                    if s == Y_SKIP and not (isinstance(row, int) and row == 0):
                        skip_term(row - 1, 1 - par)
                    if s in Y_OUT and not (isinstance(row, int) and row == 0):
                        output(row - 1, 1 - par, Y_OUT.index(s))
                    if not last:
                        front(row + 1, 1 - par, s)
                times_c(row, STEPS - 1)
            rows(body)(dve)
            skip_term(NB - 1, 1)
            for v in range(2):
                output(NB - 1, 1, v)

        @block.tensor
        def _(pe):
            M = nc.tensor.matmul
            def unit(row, u):
                if u < 2:
                    wait(pe, s_yg, (row - 1) * 2 - 1 + u)
                elif u < 4:
                    pe.wait_ge(s_xnT, row * 2 + u - 1)
                elif u == 4:
                    pe.wait_ge(s_lo, row + 1)
                elif u < 9:
                    pe.wait_ge(s_relu, row * 4 + u - 4)
                else:
                    pe.wait_ge(s_hid, row * FT + (1, 2, 4, 3)[u - 9])
                return fps[UNIT_BANK[u]]

            def transpose_xn(row, k):
                bank = unit(row, k)
                pe.wait_ge(s_xn, row * C + C)
                for c in range(C):
                    ins = nc.tensor.transpose(bank[:, c * P:(c + 1) * P], xn[:, c, k * P:(k + 1) * P], ident[:, :])
                ins.then_inc(s_pf, 1)

            def project(row, par, k):
                if k == 0:
                    unit(row, 2)
                    pe.wait_ge(s_xnT, row * 2 + 2)
                ins = M(fps[UNIT_BANK[2]][:, :], wx[:, k, :], xnT[:, par, k, :], start=(k == 0), stop=(k == DT - 1))
                if k == DT - 1:
                    ins.then_inc(s_pf, 1)

            def expand_delta(row, par, q):
                g, k = q // DT, q % DT
                bank = unit(row, 3 + q)
                if q == 0:
                    pe.wait_ge(s_dbc, row * 64 + 64)
                M(bank[:, :], dtw_high[:, g, k, :], dbc[:, par, g, :], start=True, stop=False)
                M(bank[:, :], dtw_low[:, g, k, :], dbc[:, par, g, :], start=False, stop=True).then_inc(s_pf, 1)

            def ffn_in(row, par, j, k):
                if k == 0:
                    unit(row, 7 + j)
                    pe.wait_ge(s_w, row * 64 + 64)
                ins = M(fps[UNIT_BANK[7 + j]][:, :], w1_sb[:, k, j * P:(j + 1) * P], xnT[:, par, k, :], start=(k == 0), stop=(k == DT - 1))
                if k == DT - 1:
                    ins.then_inc(s_pf, 1)

            def ffn_out(row, part):
                v, h, half = part // 4, part // 2 % 2, part % 2
                c, to = 2 * v + h, fps[UNIT_BANK[11 + v]][:, h * D:(h + 1) * D]
                if part % 4 == 0:
                    unit(row, 11 + v)
                    pe.wait_ge(s_gelu, row + 1)
                for j in range(half * 2, half * 2 + 2):
                    M(to, hT[:, j, :].rearrange("p (q c) -> p c q", c=C)[:, c, :], w2o_sb[:, j, :], start=(j == 0), stop=False)
                if half:
                    ins = M(to, ones3[:, :], bias3[:, :], start=False, stop=True)
                    if h:
                        ins.then_inc(s_pf, 1)

            def front(row, par, s):
                if s in TRANS:
                    transpose_xn(row, TRANS.index(s))
                if s in PROJECT:
                    project(row, par, PROJECT.index(s))
                if s in EXPAND:
                    expand_delta(row, par, EXPAND.index(s))
                if s in FFN_IN:
                    i = FFN_IN.index(s)
                    ffn_in(row, par, i // 2, i % 2)
                if s in FFN_OUT:
                    ffn_out(row, FFN_OUT.index(s))

            def broadcast_b(row, par, s):
                wait(pe, s_bsb, row * STEPS + s - 1)
                g, n = s // N, s % N
                M(bps[s % 2][:, :], selector[:, n:n + 1].broadcast_to([P, P]), dbc[:, par, g, :], start=True, stop=True).then_inc(s_bps, 1)

            def broadcast_c(row, par, s):
                wait(pe, s_hc, row * STEPS + s - 1)
                g, n = s // N, s % N
                M(cps[s % 2][:, :], selector[:, N + n:N + n + 1].broadcast_to([P, P]), dbc[:, par, g, :], start=True, stop=True).then_inc(s_cps, 1)

            def add_state(row, s):
                if s == 0:
                    wait(pe, s_yev, row * 2)
                pe.wait_ge(s_hc, row * STEPS + s + 1)
                for k in range(DT):
                    ins = M(yps[k][:, :], ident[:, :], hc[:, s % RING, k, :], start=(s == 0), stop=(s == STEPS - 1))
                ins.then_inc(s_red, 1)

            def tokens_of_y(row, v, last_front):
                pe.wait_ge(s_zz, last_front * 2 + 1 + v)
                pe.wait_ge(s_skip, row * DT + DT)
                for h in range(2):
                    for k in range(DT):
                        to = fps[v][:, h * D + k * P:h * D + (k + 1) * P]
                        ins = nc.tensor.transpose(to, ysb[:, k, :].rearrange("p (q c) -> p c q", c=C)[:, 2 * v + h, :], ident[:, :])
                ins.then_inc(s_y, 1)

            def product(pair):
                for a in range(2):
                    pe.wait_ge(s_w2[a], pair * 16 + 16)
                    for h in range(2):
                        for j in range(2):
                            for k in range(DT):
                                ins = nc.tensor.transpose(w2T_ps[h][:, (j * DT + k) * P:(j * DT + k + 1) * P],
                                                          w2_in[a][:, 2 * h + j, k * P:(k + 1) * P], ident[:, :])
                        ins.then_inc(s_w2T, 1)
                    for h in range(2):
                        pe.wait_ge(s_w2Tc, pair * 4 + 2 * a + h + 1)
                        wait(pe, s_w2oc, pair * 4 + 2 * a + h - 3)
                        for j in range(2):
                            for k in range(DT):
                                ins = M(w2o_ps[a][h][:, j * D:(j + 1) * D], w2T[:, 2 * h + j, k, :], wo_sb[:, k, :],
                                        start=(k == 0), stop=(k == DT - 1))
                        ins.then_inc(s_w2o, 1)

            pe.wait_ge(s_ident, 1)
            pe.wait_ge(s_wo, 16)
            for pair in range(NE // 2):
                product(pair)
                if pair == 0:
                    pe.wait_ge(s_b2T, 32)
                    pe.wait_ge(s_const, 5)
                    pe.wait_ge(s_wload, 13 * 16)
                    for k in range(DT):
                        M(bias_ps[0:NE, 0:D], b2T[:, k, :], wo_sb[:, k, :], start=(k == 0), stop=False)
                    M(bias_ps[0:NE, 0:D], ones_row[:, 0:NE], bo_row[:, :], start=False, stop=True).then_inc(s_bias, 1)
                if pair == 2:
                    pe.wait_ge(s_ra, 3)
                    for k in range(DT):
                        ins = nc.tensor.transpose(router_ps[:, k * NB:(k + 1) * NB], xnl[:, k * P:(k + 1) * P], ident[0:NB, 0:NB])
                    ins.then_inc(s_rp, 1)
            pe.wait_ge(s_rload, 5 * 16)
            pe.wait_ge(s_rv, 4)
            for k in range(DT):
                ins = M(router_ps[:, 256:256 + NB], wp1_sb[:, k, :], xlT[:, k, :], start=(k == 0), stop=(k == DT - 1))
            ins.then_inc(s_rp, 1)
            pe.wait_ge(s_w2oc, 2 * NE)
            for k in range(DT):
                nc.tensor.transpose(wx_ps[:, k * P:(k + 1) * P], xw_raw[:, k * P:(k + 1) * P], ident[:, :])
            for g in range(2):
                for k in range(DT):
                    ins = nc.tensor.transpose(dtw_ps[:, (2 * g + k) * P:(2 * g + k + 1) * P], dtw_raw[:, g, k, :], ident[:, :])
            ins.then_inc(s_wT, 1)
            pe.wait_ge(s_biasc, 2)
            for s in range(TRANS[0] + 1):
                front(0, 0, s)
            pe.wait_ge(s_ra, 4)
            M(router_ps[0:NB, 384:384 + NE], hA[:, :], wp2_sb[:, :], start=True, stop=False)
            M(router_ps[0:NB, 384:384 + NE], ones_row[:, 0:NB], bp2_row[:, :], start=False, stop=True).then_inc(s_rp, 1)
            pe.wait_ge(s_sel, 1)
            pe.wait_ge(s_wev, 3)
            pe.wait_ge(s_ra, 5)
            for s in range(TRANS[0] + 1, TRANS[1] + 1):
                front(0, 0, s)

            for s in range(TRANS[1] + 1, STEPS):
                front(0, 0, s)
            for s in range(AHEAD):
                broadcast_b(0, 0, s)
            for s in range(2):
                broadcast_c(0, 0, s)

            def body(row, par, last):
                for s in range(STEPS):
                    if s + AHEAD < STEPS:
                        broadcast_b(row, par, s + AHEAD)
                    elif not last:
                        broadcast_b(row + 1, 1 - par, s + AHEAD - STEPS)
                    front(row, par, s + STEPS)
                    if s in Y_TOKENS and not (isinstance(row, int) and row == 0):
                        tokens_of_y(row - 1, Y_TOKENS.index(s), row)
                    if not last:
                        front(row + 1, 1 - par, s)
                    if s + 2 < STEPS:
                        broadcast_c(row, par, s + 2)
                    elif not last:
                        broadcast_c(row + 1, 1 - par, s + 2 - STEPS)
                    add_state(row, s)
            rows(body)(pe)
            for v in range(2):
                tokens_of_y(NB - 1, v, NB - 1)


_INS = ["L0_attn_x", "L0_attn_x_proj_w", "L0_attn_dt_proj_w", "L0_attn_dt_proj_b", "L0_attn_A_log", "L0_attn_D",
        "L0_attn_x_proj_b_w", "L0_attn_dt_proj_b_w", "L0_attn_dt_proj_b_b", "L0_attn_A_b_log", "L0_attn_D_b",
        "L0_ffn_Wp1", "L0_ffn_bp1", "L0_ffn_Wp2", "L0_ffn_bp2", "L0_ffn_W1", "L0_ffn_b1", "L0_ffn_W2", "L0_ffn_b2",
        "L0_ffn_Wo", "L0_ffn_bo"]


def kernel(**inputs):
    import numpy as _np
    import concourse.bacc as _bacc
    from concourse.bass_utils import run_bass_kernel_spmd as _run

    nc = _bacc.Bacc("TRN2", target_bir_lowering=False, num_devices=1)
    arrays, args = {}, []
    for name in _INS:
        a = _np.ascontiguousarray(inputs[name])
        arrays[f"in_{name}_dram"] = a
        args.append(nc.dram_tensor(f"in_{name}_dram", a.shape, mybir.dt.from_np(a.dtype), kind="ExternalInput").ap())
    ne, f, d = inputs["L0_ffn_W2"].shape
    w2o = nc.dram_tensor("w2o_scratch", (ne, f, d), mybir.dt.float32, kind="Internal").ap()
    bias = nc.dram_tensor("bias_scratch", (ne, 3, d), mybir.dt.bfloat16, kind="Internal").ap()
    out = nc.dram_tensor("out_0_dram", inputs["L0_attn_x"].shape, mybir.dt.float32, kind="ExternalOutput").ap()
    mamba_moe_block(nc, *args, w2o, bias, out)
    r = _run(nc, [arrays], core_ids=[0])
    return r.results[0]["out_0_dram"]
```
